# Optimizing a Trainium2 kernel written in Bass

```python
import numpy as np
import jax
import jax.numpy as jnp

def _softmax(x, axis=-1):
    return jax.nn.softmax(x, axis=axis)

def _gelu(x):
    return jax.nn.gelu(x, approximate=True)

def _silu(x):
    return jax.nn.silu(x)

def _sigmoid(x):
    return jax.nn.sigmoid(x)

def _layernorm(x, axis=-1, eps=1e-05):
    m = jnp.mean(x, axis=axis, keepdims=True)
    v = jnp.var(x, axis=axis, keepdims=True)
    return (x - m) / jnp.sqrt(v + eps)

def _scatter_add(tgt, idx, src, axis=0):
    return tgt.at[idx].add(src)

def _segment_sum(src, seg, n):
    return jax.ops.segment_sum(src, seg, n)
kernel_name = 'mk_cond_resid_d2_seqx_r8_7426c0'

def setup_inputs(seed: int=0):
    np.random.seed(seed)
    _w = jnp.asarray

    def _rec_inputs():
        import jax
        import jax.numpy as jnp
        _rk = jax.random.key(seed)
        x = -0.000125 + 0.9999 * jax.random.normal(jax.random.fold_in(_rk, 1), (64, 32, 512), jnp.float32)
        _lenS = 32 - jax.random.randint(jax.random.fold_in(_rk, 7), (64,), 0, max(1, 32 // 4) + 1, jnp.int32)
        _lenS2 = 32 - jax.random.randint(jax.random.fold_in(_rk, 8), (64,), 0, max(1, 32 // 4) + 1, jnp.int32)
        itok_B_0_7 = jax.random.randint(jax.random.fold_in(_rk, 11), (64,), 0, 8, jnp.int32)
        itok_B_4_50 = jax.random.randint(jax.random.fold_in(_rk, 12), (64,), 4, 51, jnp.int32)
        return (x, itok_B_0_7, itok_B_4_50)
    x, itok_B_0_7, itok_B_4_50 = _rec_inputs()

    def _L0_cond_setup():
        import jax, jax.numpy as jnp
        import numpy as np
        TOP_K = 2
        LANG_BIAS = 5.0
        SCALING = 32.0 / 16.0
        LANGUAGE_PAD_ID = -1
        key = jax.random.key(seed)
        ks = jax.random.split(key, 6)
        B, T, D, O, E, R = (4, 256, 512, 512, 8, 16)
        x = jax.random.normal(ks[0], (B, T, D), dtype=jnp.float32)
        language_ids = jax.random.randint(ks[1], (B,), 0, E).astype(jnp.int64)
        W = jax.random.normal(ks[2], (O, D), dtype=jnp.float32) * (1.0 / np.sqrt(D))
        Wr = jax.random.normal(ks[3], (E, D), dtype=jnp.float32) * (1.0 / np.sqrt(D))
        A = jax.random.normal(ks[4], (E, R, D), dtype=jnp.float32) * (1.0 / np.sqrt(D))
        Bm = jax.random.normal(ks[5], (O, R), dtype=jnp.float32) * 0.0
        Bm = jnp.broadcast_to(Bm, (E, O, R)) + jax.random.normal(ks[5], (E, O, R), dtype=jnp.float32) * 0.02
        return {'x': x, 'language_ids': language_ids, 'W': W, 'Wr': Wr, 'A': A, 'B': Bm}
    _L0_cond_all = _L0_cond_setup()
    _L0_cond_in = {k: v for k, v in _L0_cond_all.items() if k in ('W', 'Wr', 'A', 'B')}
    del _L0_cond_all

    def _L1_cond_setup():
        import jax, jax.numpy as jnp
        import numpy as np
        RANK = 16
        ALPHA = 16.0
        SCALING = ALPHA / RANK
        key = jax.random.key(seed)
        k1, k2, k3, k4 = jax.random.split(key, 4)
        batch, n_tok, d_in, d_out, n_adapters, rank = (8, 256, 512, 512, 64, RANK)
        x = jax.random.normal(k1, (batch, n_tok, d_in), dtype=jnp.float32)
        A = jax.random.normal(k2, (n_adapters, d_out, rank), dtype=jnp.float32) * 0.02
        B = jax.random.normal(k3, (n_adapters, rank, d_in), dtype=jnp.float32)
        adapter_ids = jax.random.randint(k4, (batch,), 0, n_adapters, dtype=jnp.int32)
        return {'x': x, 'A': A, 'B': B, 'adapter_ids': adapter_ids}
    _L1_cond_all = _L1_cond_setup()
    _L1_cond_in = {k: v for k, v in _L1_cond_all.items() if k in ('A', 'B')}
    del _L1_cond_all
    return {'x': x, 'itok_B_0_7': itok_B_0_7, 'itok_B_4_50': itok_B_4_50, 'L0_cond_W': _L0_cond_in['W'], 'L0_cond_Wr': _L0_cond_in['Wr'], 'L0_cond_A': _L0_cond_in['A'], 'L0_cond_B': _L0_cond_in['B'], 'L1_cond_A': _L1_cond_in['A'], 'L1_cond_B': _L1_cond_in['B']}

def reference(x, itok_B_0_7, itok_B_4_50, L0_cond_W, L0_cond_Wr, L0_cond_A, L0_cond_B, L1_cond_A, L1_cond_B):
    import jax
    import jax.numpy as jnp

    def _L0_cond_ref(x, language_ids, W, Wr, A, B):
        import jax, jax.numpy as jnp
        import numpy as np
        TOP_K = 2
        LANG_BIAS = 5.0
        SCALING = 32.0 / 16.0
        LANGUAGE_PAD_ID = -1
        base = jnp.einsum('btd,od->bto', x, W)
        E = Wr.shape[0]
        logits = jnp.einsum('btd,ed->bte', x.astype(jnp.float32), Wr.astype(jnp.float32))
        expert_targets = language_ids
        valid = expert_targets >= 0
        tgt = jnp.where(valid, expert_targets, 0)
        bias = jax.nn.one_hot(tgt, E, dtype=logits.dtype) * LANG_BIAS
        bias = jnp.where(valid[:, None], bias, 0.0)
        logits = logits + bias[:, None, :]
        topw, topi = jax.lax.top_k(logits, TOP_K)
        weights = jax.nn.softmax(topw, axis=-1)
        gates = jnp.sum(jax.nn.one_hot(topi, E, dtype=weights.dtype) * weights[..., None], axis=-2)
        gates = gates.astype(x.dtype)
        h = jnp.einsum('btd,erd->bter', x, A)
        lora_out = jnp.einsum('bter,bte,eor->bto', h, gates, B)
        return base + SCALING * lora_out

    def _L1_cond_ref(x, A, B, adapter_ids):
        import jax, jax.numpy as jnp
        import numpy as np
        RANK = 16
        ALPHA = 16.0
        SCALING = ALPHA / RANK
        B_req = B[adapter_ids]
        A_req = A[adapter_ids]
        Bx = jnp.einsum('bni,bri->bnr', x, B_req)
        out = jnp.einsum('bnr,bor->bno', Bx, A_req)
        return out * SCALING
    x = x + _L0_cond_ref(x, itok_B_0_7, L0_cond_W, L0_cond_Wr, L0_cond_A, L0_cond_B)
    x = x + _L1_cond_ref(x, L1_cond_A, L1_cond_B, itok_B_4_50)
    return x

_drawn_inputs = setup_inputs


def setup_inputs(seed=0):
    import zlib

    import numpy as np

    out = dict(_drawn_inputs(seed))
    spreads = {}
    factors = {'L0_cond_Wr': 5.082}
    for name, (base, spread) in spreads.items():
        noise = np.random.default_rng([zlib.crc32(name.encode()), seed]).standard_normal(out[name].shape)
        drawn = base * np.exp(spread * noise) if base else spread * noise
        out[name] = jnp.asarray(drawn.astype(out[name].dtype))
    for name, factor in factors.items():
        out[name] = (out[name] * factor).astype(out[name].dtype)
    return out
```

```python
from contextlib import ExitStack

import concourse.bass as bass
from concourse import mybir

P = 128
F32 = mybir.dt.float32
F32R = mybir.dt.float32r
I32 = mybir.dt.int32
U32 = mybir.dt.uint32
ALU = mybir.AluOpType
ACT = mybir.ActivationFunctionType

LANG_BIAS = 5.0
SCALING0 = 32.0 / 16.0


def two_block_kernel(nc, x, adapter_id, language_id, w, aw, b0, table, out, *, tokens_per_batch, experts,
                     rank, adapters):
    _, NB, K, TB = x.shape
    D = K * P
    AWN = aw.shape[2]
    H = experts * rank
    TILES = TB // P
    BPG = P // rank
    GT = BPG * tokens_per_batch
    GPB = TB // GT
    NG = NB * GPB
    assert H == P and GPB == 2 and K == 4 and TILES == 4 and 2 * AWN <= 512
    SLOTS = 2 * GPB

    with ExitStack() as ctx:
        def sb(name, shape, dt=F32):
            return ctx.enter_context(nc.sbuf_tensor(name, shape, dt))

        def psum(name):
            return ctx.enter_context(nc.psum_tensor(name, [P, 512], F32))

        def sem(name):
            return ctx.enter_context(nc.semaphore(name))

        xs = sb("xs", [P, NB, K, TB])
        x_hi, x_lo = sb("x_hi", [P, 2, K, TB], F32R), sb("x_lo", [P, 2, K, TB], F32R)
        x1_hi, x1_lo = sb("x1_hi", [P, K, TB], F32R), sb("x1_lo", [P, K, TB], F32R)
        ws = sb("ws", [P, K, K, P])
        w_hi, w_lo = sb("w_hi", [P, K, K, P], F32R), sb("w_lo", [P, K, K, P], F32R)
        aws = sb("aws", [P, K, AWN])
        aw_hl = sb("aw_hl", [P, K, 2, AWN], F32R)
        b0s = sb("b0s", [P, D])
        b0_hi, b0_lo = sb("b0_hi", [P, D], F32R), sb("b0_lo", [P, D], F32R)
        rows = sb("rows", [P, SLOTS, 2, D])
        a1_hi, a1_lo = sb("a1_hi", [P, SLOTS, D], F32R), sb("a1_lo", [P, SLOTS, D], F32R)
        bt_hi, bt_lo = sb("bt_hi", [P, GPB, K, P], F32R), sb("bt_lo", [P, GPB, K, P], F32R)
        aw_rest = sb("aw_rest", [P, 2, AWN])
        hw = sb("hw", [P, TILES, AWN])
        logits = sb("logits", [P, TILES, experts])
        top = sb("top", [P, TILES, 8])
        top_at = sb("top_at", [P, TILES, 8], U32)
        gap = sb("gap", [P, TILES])
        gap_exp = sb("gap_exp", [P, TILES])
        denom = sb("denom", [P, TILES])
        inv = sb("inv", [P, TILES])
        weight = sb("weight", [P, TILES, 2])
        picked = sb("picked", [P, TILES, 2, experts])
        picked_w = sb("picked_w", [P, TILES, 2, experts])
        gate = sb("gate", [P, TILES, experts])
        gated = sb("gated", [P, TILES, H])
        gt_hi, gt_lo = sb("gt_hi", [P, TB], F32R), sb("gt_lo", [P, TB], F32R)
        down = sb("down", [P, GPB, GT])
        down_hi, down_lo = sb("down_hi", [P, GPB, GT], F32R), sb("down_lo", [P, GPB, GT], F32R)
        ident = sb("ident", [P, P])
        own_batch = sb("own_batch", [P, BPG])
        expert_no = sb("expert_no", [P, experts])
        part_no = sb("part_no", [P, 1], I32)
        rank_no = sb("rank_no", [P, 1], I32)
        adapter_ids = sb("adapter_ids", [P, NG], I32)
        wrap = sb("wrap", [P, NG], I32)
        wrapped = sb("wrapped", [P, NG], I32)
        clamped = sb("clamped", [P, NG], I32)
        row_at = sb("row_at", [P, NG], I32)
        language_ids = sb("language_ids", [P, NB, TILES], I32)
        is_language = sb("is_language", [P, NB, TILES, experts])
        bias = sb("bias", [P, NB, TILES, experts])

        main = [psum(f"main{i}") for i in range(4)]
        aw_ps = [psum(f"aw_ps{i}") for i in range(2)]
        side = [psum(f"side{i}") for i in range(2)]

        ids_loaded = sem("ids_loaded")
        x0_loaded = [sem(f"x0_loaded{c}") for c in range(K)]
        x_loaded = [None] + [sem(f"x_loaded{t}") for t in range(1, NB)]
        w_loaded = [sem(f"w_loaded{c}") for c in range(K)]
        aw_loaded, b0_loaded = sem("aw_loaded"), sem("b0_loaded")
        rows_loaded = [sem(f"rows_loaded{g}") for g in range(NG)]
        stored = sem("stored")
        const_step, const_ready = sem("const_step"), sem("const_ready")
        x_lo_ready, a1_lo_ready = sem("x_lo_ready"), sem("a1_lo_ready")
        w_hi_ready, aw_hi_ready, b0_hi_ready = sem("w_hi_ready"), sem("aw_hi_ready"), sem("b0_hi_ready")
        x_hi_ready, a1_hi_ready, x1_hi_ready = sem("x_hi_ready"), sem("a1_hi_ready"), sem("x1_hi_ready")
        bt_hi_ready, gt_hi_ready, down_hi_ready = sem("bt_hi_ready"), sem("gt_hi_ready"), sem("down_hi_ready")
        rest_ready, exp_ready = sem("rest_ready"), sem("exp_ready")
        w_lo_ready, aw_lo_ready, b0_lo_ready = sem("w_lo_ready"), sem("aw_lo_ready"), sem("b0_lo_ready")
        x0_lo_ready, x1_ready, x1_lo_ready = sem("x0_lo_ready"), sem("x1_ready"), sem("x1_lo_ready")
        bt_lo_ready, gt_lo_ready = sem("bt_lo_ready"), sem("gt_lo_ready")
        down_ready, down_lo_ready = sem("down_ready"), sem("down_lo_ready")
        hw_ready, gap_ready, gated_ready = sem("hw_ready"), sem("gap_ready"), sem("gated_ready")
        x2_ready, row_at_ready = sem("x2_ready"), sem("row_at_ready")
        vector_step = sem("vector_step")
        aw_done, base_done, lora_done = sem("aw_done"), sem("base_done"), sem("lora_done")
        gt_done, bt_done, down_done, up_done = sem("gt_done"), sem("bt_done"), sem("down_done"), sem("up_done")

        def up_bank(t, c):
            return c if t == NB - 1 else (1, 2, 3, 1)[c]

        block = ctx.enter_context(nc.Block())

        @block.sync
        def _(sp):
            for c in range(K):
                sp.dma_start(xs[:, 0, c, :], x[:, 0, c, :]).then_inc(x0_loaded[c], 16)
            sp.dma_start(aws[:], aw).then_inc(aw_loaded, 16)
            for c in range(1, K):
                sp.dma_start(ws[:, c], w[:, c]).then_inc(w_loaded[c], 16)
            for t in range(1, NB):
                sp.dma_start(xs[:, t], x[:, t]).then_inc(x_loaded[t], 16)
            for t in range(NB):
                for c in range(K):
                    sp.wait_ge(x2_ready, t * K + c + 1)
                    sp.dma_start(out[:, t, c, :], xs[:, t, c, :]).then_inc(stored, 16)
            sp.wait_ge(stored, 16 * NB * K)

        @block.gpsimd
        def _(pool):
            nc.gpsimd.iota(part_no[:], [[0, 1]], base=0, channel_multiplier=1).then_inc(const_ready, 1)
            nc.gpsimd.iota(expert_no[:], [[1, experts]], base=0, channel_multiplier=0,
                           allow_small_or_imprecise_dtypes=True).then_inc(const_ready, 1)
            nc.gpsimd.memset(ident[:], 0.0).then_inc(const_step, 1)
            nc.gpsimd.memset(own_batch[:], 1.0).then_inc(const_step, 1)
            pool.wait_ge(const_step, 2)
            nc.gpsimd.affine_select(out=ident[:], in_=ident[:], compare_op=ALU.not_equal, fill=1.0, base=0,
                                    pattern=[[-1, P]], channel_multiplier=1).then_inc(const_ready, 1)
            nc.gpsimd.affine_select(out=own_batch[:], in_=own_batch[:], compare_op=ALU.is_ge, fill=0.0, base=0,
                                    pattern=[[-rank, BPG]], channel_multiplier=1).then_inc(const_step, 1)
            pool.wait_ge(const_step, 3)
            nc.gpsimd.affine_select(out=own_batch[:], in_=own_batch[:], compare_op=ALU.is_ge, fill=0.0,
                                    base=rank - 1, pattern=[[rank, BPG]],
                                    channel_multiplier=-1).then_inc(const_ready, 1)

            def gather(g):
                if g >= SLOTS:
                    pool.wait_ge(a1_hi_ready, g - SLOTS + 1)
                    pool.wait_ge(a1_lo_ready, g - SLOTS + 1)
                    pool.wait_ge(bt_done, g - SLOTS + 1)
                nc.gpsimd.indirect_dma_start(
                    rows[:, g % SLOTS].rearrange("p a d -> p (a d)"), None, table,
                    bass.IndirectOffsetOnAxis(ap=row_at[:, g:g + 1], axis=0)).then_inc(rows_loaded[g], 16)

            def split_a1(g):
                pool.wait_ge(a1_hi_ready, g + 1)
                if g >= SLOTS:
                    pool.wait_ge(up_done, K * (g // GPB - 1))
                s = g % SLOTS
                nc.gpsimd.tensor_tensor(a1_lo[:, s], rows[:, s, 1], a1_hi[:, s].bitcast(F32),
                                        ALU.subtract).then_inc(a1_lo_ready, 1)

            pool.wait_ge(row_at_ready, 1)
            for g in range(SLOTS):
                gather(g)
            for t in range(NB):
                if t >= 1:
                    for c in range(K):
                        pool.wait_ge(x_hi_ready, t * K + c + 1)
                        if t >= 2 and c == 0:
                            pool.wait_ge(base_done, (t - 1) * K)
                        nc.gpsimd.tensor_tensor(x_lo[:, t % 2, c], xs[:, t, c], x_hi[:, t % 2, c].bitcast(F32),
                                                ALU.subtract).then_inc(x_lo_ready, 1)
                for g in range(t * GPB, (t + 1) * GPB):
                    split_a1(g)
                    if g >= 1 and g - 1 + SLOTS < NG:
                        gather(g - 1 + SLOTS)

        @block.scalar
        def _(act):
            act.dma_start(ws[:, 0], w[:, 0]).then_inc(w_loaded[0], 16)
            act.dma_start(adapter_ids[:], adapter_id).then_inc(ids_loaded, 16)
            act.dma_start(language_ids[:], language_id.rearrange("p (t j) -> p t j", t=NB)).then_inc(ids_loaded, 16)
            act.dma_start(b0s[:], b0).then_inc(b0_loaded, 16)

            def round_hi(dst, src, ready):
                nc.scalar.activation(dst, src, ACT.Copy).then_inc(ready, 1)

            def w_half(c):
                act.wait_ge(w_loaded[c], 16)
                round_hi(w_hi[:, c], ws[:, c], w_hi_ready)

            def x_half(t, c):
                if t == 0:
                    act.wait_ge(x0_loaded[c], 16)
                elif c == 0:
                    act.wait_ge(x_loaded[t], 16)
                    if t >= 2:
                        act.wait_ge(base_done, (t - 1) * K)
                round_hi(x_hi[:, t % 2, c], xs[:, t, c], x_hi_ready)

            def a1_half(g):
                act.wait_ge(rows_loaded[g], 16)
                if g >= SLOTS:
                    act.wait_ge(up_done, K * (g // GPB - 1))
                round_hi(a1_hi[:, g % SLOTS], rows[:, g % SLOTS, 1], a1_hi_ready)

            def copy_rest(u, j):
                n = u * TILES + j
                act.wait_ge(aw_done, n + 1)
                if n >= 2:
                    act.wait_ge(hw_ready, n - 1)
                nc.scalar.activation(aw_rest[:, n % 2], aw_ps[n % 2][:, AWN:2 * AWN], ACT.Copy).then_inc(rest_ready, 1)

            def exp_gap(u):
                act.wait_ge(gap_ready, u + 1)
                nc.scalar.activation(gap_exp[:], gap[:], ACT.Exp).then_inc(exp_ready, 1)

            def gt_half(u):
                act.wait_ge(gt_done, u + 1)
                if u >= 1:
                    act.wait_ge(lora_done, u * K)
                round_hi(gt_hi[:], side[1][:], gt_hi_ready)

            def bt_half(g):
                act.wait_ge(bt_done, g + 1)
                if g >= GPB:
                    act.wait_ge(down_done, g - GPB + 1)
                round_hi(bt_hi[:, g % GPB].rearrange("p k m -> p (k m)"), side[g % 2][:], bt_hi_ready)

            def x1_half(t, c):
                act.wait_ge(x1_ready, t * K + c + 1)
                if t >= 1:
                    act.wait_ge(down_done, t * GPB)
                round_hi(x1_hi[:, c], xs[:, t, c], x1_hi_ready)

            def down_half(g):
                act.wait_ge(down_ready, g + 1)
                if g >= GPB:
                    act.wait_ge(up_done, K * (g // GPB))
                round_hi(down_hi[:, g % GPB], down[:, g % GPB], down_hi_ready)

            w_half(0)
            for c in range(K):
                x_half(0, c)
            act.wait_ge(aw_loaded, 16)
            round_hi(aw_hl[:, :, 0], aws[:], aw_hi_ready)
            w_half(1)
            for j in range(TILES):
                copy_rest(0, j)
            act.wait_ge(b0_loaded, 16)
            round_hi(b0_hi[:], b0s[:], b0_hi_ready)
            exp_gap(0)
            bt_half(0)
            w_half(2)
            gt_half(0)
            w_half(3)
            x1_half(0, 0)
            a1_half(0)
            x1_half(0, 1)
            a1_half(1)
            bt_half(1)
            x1_half(0, 2)
            for c in range(K):
                x_half(1, c)
            x1_half(0, 3)
            for t in range(NB):
                more = t + 1 < NB
                if more:
                    for j in range(TILES):
                        copy_rest(t + 1, j)
                    exp_gap(t + 1)
                for g in range(t * GPB, (t + 1) * GPB):
                    down_half(g)
                if more:
                    gt_half(t + 1)
                    a1_half((t + 1) * GPB)
                    if t + 2 < NB:
                        for c in range(K):
                            x_half(t + 2, c)
                    x1_half(t + 1, 0)
                    bt_half((t + 1) * GPB)
                    a1_half((t + 1) * GPB + 1)
                    x1_half(t + 1, 1)
                    bt_half((t + 1) * GPB + 1)
                    x1_half(t + 1, 2)
                    x1_half(t + 1, 3)

        @block.vector
        def _(dve):
            steps = [0]

            def then_wait(instruction):
                steps[0] += 1
                instruction.then_inc(vector_step, 1)
                dve.wait_ge(vector_step, steps[0])

            def split_lo(dst, src, hi, ready):
                nc.vector.tensor_tensor(dst, src, hi.bitcast(F32), ALU.subtract).then_inc(ready, 1)

            def w_rest(c):
                dve.wait_ge(w_hi_ready, c + 1)
                split_lo(w_lo[:, c], ws[:, c], w_hi[:, c], w_lo_ready)

            def add_rest(u, j):
                n = u * TILES + j
                dve.wait_ge(rest_ready, n + 1)
                nc.vector.tensor_tensor(hw[:, j], aw_ps[n % 2][:, 0:AWN], aw_rest[:, n % 2],
                                        ALU.add).then_inc(hw_ready, 1)

            def top_two(u):
                dve.wait_ge(hw_ready, (u + 1) * TILES)
                then_wait(nc.vector.tensor_tensor(logits[:], hw[:, :, H:AWN], bias[:, u], ALU.add))
                for j in range(TILES):
                    last = nc.vector.max(top[:, j], logits[:, j])
                then_wait(last)
                nc.vector.tensor_tensor(gap[:], top[:, :, 1], top[:, :, 0], ALU.subtract).then_inc(gap_ready, 1)
                for j in range(TILES):
                    last = nc.vector.max_index(top_at[:, j], top[:, j], logits[:, j])
                then_wait(last)

            def gate_h(u):
                dve.wait_ge(exp_ready, u + 1)
                then_wait(nc.vector.tensor_scalar(denom[:], gap_exp[:], 1.0, None, ALU.add))
                then_wait(nc.vector.reciprocal(inv[:], denom[:]))
                nc.vector.tensor_scalar(weight[:, :, 0], inv[:], SCALING0, None, ALU.mult)
                then_wait(nc.vector.scalar_tensor_tensor(weight[:, :, 1], gap_exp[:], SCALING0, inv[:],
                                                         ALU.mult, ALU.mult))
                then_wait(nc.vector.tensor_tensor(
                    picked_w[:], picked[:], weight[:].unsqueeze(3).broadcast_to([P, TILES, 2, experts]), ALU.mult))
                then_wait(nc.vector.tensor_tensor(gate[:], picked_w[:, :, 0], picked_w[:, :, 1], ALU.add))
                if u >= 1:
                    dve.wait_ge(gt_done, u)
                nc.vector.tensor_tensor(
                    gated[:].rearrange("p j (e r) -> p j e r", e=experts),
                    hw[:, :, 0:H].rearrange("p j (e r) -> p j e r", e=experts),
                    gate[:].unsqueeze(3).broadcast_to([P, TILES, experts, rank]), ALU.mult).then_inc(gated_ready, 1)

            def pick():
                then_wait(nc.vector.tensor_tensor(
                    picked[:], top_at[:, :, 0:2].unsqueeze(3).broadcast_to([P, TILES, 2, experts]),
                    expert_no[:].unsqueeze(1).unsqueeze(1).broadcast_to([P, TILES, 2, experts]), ALU.is_equal))

            def add_x1(t, c):
                dve.wait_ge(lora_done, t * K + c + 1)
                nc.vector.tensor_tensor(xs[:, t, c], main[c][:], xs[:, t, c], ALU.add).then_inc(x1_ready, 1)

            def x1_rest(t, c):
                dve.wait_ge(x1_hi_ready, t * K + c + 1)
                split_lo(x1_lo[:, c], xs[:, t, c], x1_hi[:, c], x1_lo_ready)

            def mask_down(g):
                dve.wait_ge(down_done, g + 1)
                nc.vector.tensor_tensor(
                    down[:, g % GPB].rearrange("p (b n) -> p b n", b=BPG),
                    side[g % 2][:, 0:GT].rearrange("p (b n) -> p b n", b=BPG),
                    own_batch[:].unsqueeze(2).broadcast_to([P, BPG, tokens_per_batch]),
                    ALU.mult).then_inc(down_ready, 1)

            def down_rest(g):
                dve.wait_ge(down_hi_ready, g + 1)
                split_lo(down_lo[:, g % GPB], down[:, g % GPB], down_hi[:, g % GPB], down_lo_ready)

            def gt_rest(u):
                dve.wait_ge(gt_hi_ready, u + 1)
                split_lo(gt_lo[:], side[1][:], gt_hi[:], gt_lo_ready)

            def bt_rest(g):
                dve.wait_ge(bt_hi_ready, g + 1)
                split_lo(bt_lo[:, g % GPB].rearrange("p k m -> p (k m)"), side[g % 2][:],
                         bt_hi[:, g % GPB].rearrange("p k m -> p (k m)"), bt_lo_ready)

            def add_x2(t, c):
                dve.wait_ge(up_done, t * K + c + 1)
                nc.vector.tensor_tensor(xs[:, t, c], main[up_bank(t, c)][:], xs[:, t, c],
                                        ALU.add).then_inc(x2_ready, 1)

            dve.wait_ge(const_ready, 2)
            dve.wait_ge(ids_loaded, 32)
            then_wait(nc.vector.tensor_scalar(rank_no[:], part_no[:], rank - 1, None, ALU.bitwise_and))
            then_wait(nc.vector.tensor_scalar(wrap[:], adapter_ids[:], 0.0, float(adapters), ALU.is_lt, ALU.mult))
            then_wait(nc.vector.tensor_tensor(wrapped[:], wrap[:], adapter_ids[:], ALU.add))
            then_wait(nc.vector.tensor_scalar(clamped[:], wrapped[:], 0.0, float(adapters - 1), ALU.max, ALU.min))
            nc.vector.scalar_tensor_tensor(row_at[:], clamped[:], float(rank), rank_no[:].broadcast_to([P, NG]),
                                           ALU.mult, ALU.add).then_inc(row_at_ready, 1)
            then_wait(nc.vector.tensor_tensor(
                is_language[:].rearrange("p t j e -> p (t j) e"),
                language_ids[:].rearrange("p t j -> p (t j)").unsqueeze(2).broadcast_to([P, NB * TILES, experts]),
                expert_no[:].unsqueeze(1).broadcast_to([P, NB * TILES, experts]), ALU.is_equal))
            then_wait(nc.vector.tensor_scalar(bias[:], is_language[:], LANG_BIAS, None, ALU.mult))

            w_rest(0)
            for c in range(K):
                dve.wait_ge(x_hi_ready, c + 1)
                split_lo(x_lo[:, 0, c], xs[:, 0, c], x_hi[:, 0, c], x0_lo_ready)
            dve.wait_ge(aw_hi_ready, 1)
            split_lo(aw_hl[:, :, 1], aws[:], aw_hl[:, :, 0], aw_lo_ready)
            w_rest(1)
            for j in range(TILES):
                add_rest(0, j)
            dve.wait_ge(b0_hi_ready, 1)
            split_lo(b0_lo[:], b0s[:], b0_hi[:], b0_lo_ready)
            top_two(0)
            pick()
            gate_h(0)
            bt_rest(0)
            w_rest(2)
            gt_rest(0)
            w_rest(3)
            dve.wait_ge(const_ready, 4)
            for c in range(K):
                add_x1(0, c)
                x1_rest(0, c)
                if c == 1:
                    bt_rest(1)
            for t in range(NB):
                more = t + 1 < NB
                if more:
                    for j in range(TILES):
                        add_rest(t + 1, j)
                    top_two(t + 1)
                    pick()
                    gate_h(t + 1)
                for g in range(t * GPB, (t + 1) * GPB):
                    mask_down(g)
                for g in range(t * GPB, (t + 1) * GPB):
                    down_rest(g)
                if more:
                    gt_rest(t + 1)
                for c in range(K):
                    add_x2(t, c)
                if more:
                    for c in range(K):
                        add_x1(t + 1, c)
                        x1_rest(t + 1, c)
                        if c < GPB:
                            bt_rest((t + 1) * GPB + c)

        @block.tensor
        def _(pe):
            def three(out_ap, terms):
                for i, (lhsT, rhs) in enumerate(terms):
                    last = nc.tensor.matmul(out_ap, lhsT, rhs, start=(i == 0), stop=(i == len(terms) - 1))
                return last

            def base(t, c):
                s = t % 2
                pe.wait_ge(w_hi_ready, c + 1)
                pe.wait_ge(w_lo_ready, c + 1)
                if t >= 1:
                    if c == 0:
                        pe.wait_ge(x1_ready, (t - 1) * K + 1)
                    else:
                        pe.wait_ge(x2_ready, (t - 1) * K + (K if c == 1 else c))
                for k in range(K):
                    if t == 0 and c == 0:
                        pe.wait_ge(x_hi_ready, k + 1)
                    first = nc.tensor.matmul(main[c][:], w_hi[:, c, k], x_hi[:, s, k], start=(k == 0), stop=False)
                    nc.tensor.matmul(main[c][:], w_lo[:, c, k], x_hi[:, s, k], start=False, stop=False)
                    if t == 0 and c == 0:
                        pe.wait_ge(x0_lo_ready, k + 1)
                    last = nc.tensor.matmul(main[c][:], w_hi[:, c, k], x_lo[:, s, k], start=False, stop=False)
                last.then_inc(base_done, 1)

            def lora(t, c):
                if c == 0:
                    pe.wait_ge(gt_hi_ready, t + 1)
                    pe.wait_ge(gt_lo_ready, t + 1)
                    pe.wait_ge(b0_hi_ready, 1)
                    pe.wait_ge(b0_lo_ready, 1)
                m = slice(c * P, (c + 1) * P)
                nc.tensor.matmul(main[c][:], b0_hi[:, m], gt_hi[:], start=False, stop=False)
                nc.tensor.matmul(main[c][:], b0_lo[:, m], gt_hi[:], start=False, stop=False)
                nc.tensor.matmul(main[c][:], b0_hi[:, m], gt_lo[:], start=False, stop=True).then_inc(lora_done, 1)

            def aw_tiles(u):
                s = u % 2
                pe.wait_ge(aw_hi_ready, 1)
                pe.wait_ge(aw_lo_ready, 1)
                if u >= 1:
                    pe.wait_ge(x_hi_ready, (u + 1) * K)
                    pe.wait_ge(x_lo_ready, u * K)
                for j in range(TILES):
                    n = u * TILES + j
                    if n >= 2:
                        pe.wait_ge(hw_ready, n - 1)
                    m = slice(j * P, (j + 1) * P)
                    for k in range(K):
                        nc.tensor.matmul(aw_ps[n % 2][:, 0:2 * AWN], x_hi[:, s, k, m],
                                         aw_hl[:, k].rearrange("p h n -> p (h n)"), start=(k == 0), stop=False)
                        last = nc.tensor.matmul(aw_ps[n % 2][:, 0:AWN], x_lo[:, s, k, m], aw_hl[:, k, 0],
                                                start=False, stop=(k == K - 1))
                    last.then_inc(aw_done, 1)

            def gt_transposes(u):
                pe.wait_ge(gated_ready, u + 1)
                if u >= 1:
                    pe.wait_ge(down_ready, u * GPB)
                for j in range(TILES):
                    last = nc.tensor.transpose(side[1][:, j * P:(j + 1) * P], gated[:, j], ident[:])
                last.then_inc(gt_done, 1)

            def bt_transposes(g):
                pe.wait_ge(rows_loaded[g], 16)
                if g == 0:
                    pe.wait_ge(const_ready, 3)
                if g % 2 == 1:
                    pe.wait_ge(gt_lo_ready, g // 2 + 1)
                elif g >= 2:
                    pe.wait_ge(down_ready, g - 1)
                for k in range(K):
                    last = nc.tensor.transpose(side[g % 2][:, k * P:(k + 1) * P],
                                               rows[:, g % SLOTS, 0, k * P:(k + 1) * P], ident[:])
                last.then_inc(bt_done, 1)

            def down_group(g):
                t, s = g // GPB, g % GPB
                n = slice(s * GT, (s + 1) * GT)
                pe.wait_ge(bt_hi_ready, g + 1)
                pe.wait_ge(bt_lo_ready, g + 1)
                terms = []
                for k in range(K):
                    terms += [(bt_hi[:, s, k], x1_hi[:, k, n]), (bt_lo[:, s, k], x1_hi[:, k, n]),
                              (bt_hi[:, s, k], x1_lo[:, k, n])]
                pe.wait_ge(x1_hi_ready, (t + 1) * K)
                pe.wait_ge(x1_lo_ready, (t + 1) * K)
                three(side[g % 2][:, 0:GT], terms).then_inc(down_done, 1)

            def up(t, c):
                bank = main[up_bank(t, c)]
                if t < NB - 1:
                    if c < K - 1:
                        pe.wait_ge(x1_ready, t * K + c + 2)
                    else:
                        pe.wait_ge(x2_ready, t * K + 1)
                else:
                    pe.wait_ge(x1_ready, t * K + c + 1)
                m = slice(c * P, (c + 1) * P)
                for g in range(t * GPB, (t + 1) * GPB):
                    s, a = g % GPB, g % SLOTS
                    if c == 0:
                        pe.wait_ge(a1_lo_ready, g + 1)
                        pe.wait_ge(down_lo_ready, g + 1)
                    last = three(bank[:, s * GT:(s + 1) * GT],
                                 [(a1_hi[:, a, m], down_hi[:, s]), (a1_lo[:, a, m], down_hi[:, s]),
                                  (a1_hi[:, a, m], down_lo[:, s])])
                last.then_inc(up_done, 1)

            base(0, 0)
            aw_tiles(0)
            bt_transposes(0)
            base(0, 1)
            gt_transposes(0)
            lora(0, 0)
            lora(0, 1)
            bt_transposes(1)
            base(0, 2)
            lora(0, 2)
            base(0, 3)
            lora(0, 3)
            for t in range(NB):
                more = t + 1 < NB
                if more:
                    aw_tiles(t + 1)
                for g in range(t * GPB, (t + 1) * GPB):
                    down_group(g)
                if more:
                    base(t + 1, 0)
                    gt_transposes(t + 1)
                for c in range(K):
                    up(t, c)
                if more:
                    lora(t + 1, 0)
                    bt_transposes((t + 1) * GPB)
                    base(t + 1, 1)
                    lora(t + 1, 1)
                    bt_transposes((t + 1) * GPB + 1)
                    for c in range(2, K):
                        base(t + 1, c)
                        lora(t + 1, c)


def kernel(x, itok_B_0_7, itok_B_4_50, L0_cond_W, L0_cond_Wr, L0_cond_A, L0_cond_B, L1_cond_A, L1_cond_B):
    import numpy as np
    import concourse.bacc as bacc
    from concourse.bass_utils import run_bass_kernel_spmd

    x, w, wr, a0, b0, a1, b1 = (np.asarray(v) for v in (
        x, L0_cond_W, L0_cond_Wr, L0_cond_A, L0_cond_B, L1_cond_A, L1_cond_B))
    adapter, language = np.asarray(itok_B_4_50), np.asarray(itok_B_0_7)
    B, T, D = x.shape
    E, R, _ = a0.shape
    NA = a1.shape[0]
    K, TB = D // P, 512
    NB = B * T // TB
    arrays = {
        "x_t": x.reshape(NB, TB, K, P).transpose(3, 0, 2, 1),
        "adapter_id": np.repeat(adapter.reshape(-1, P // R).T, R, axis=0),
        "language_id": np.repeat(language.reshape(-1, P // T).T, T, axis=0),
        "w_t": w.reshape(K, P, K, P).transpose(3, 0, 2, 1),
        "aw_t": np.concatenate([a0.reshape(E * R, D), wr]).T.reshape(K, P, -1).transpose(1, 0, 2),
        "b0_t": b0.transpose(0, 2, 1).reshape(E * R, D),
        "table": np.concatenate([b1.reshape(NA * R, D), a1.transpose(0, 2, 1).reshape(NA * R, D)], axis=1),
    }
    arrays = {k: np.ascontiguousarray(v) for k, v in arrays.items()}

    nc = bacc.Bacc("TRN2", target_bir_lowering=False, num_devices=1)
    aps = [nc.dram_tensor(k, v.shape, mybir.dt.from_np(v.dtype), kind="ExternalInput").ap() for k, v in arrays.items()]
    out = nc.dram_tensor("out_t", arrays["x_t"].shape, F32, kind="ExternalOutput").ap()
    two_block_kernel(nc, *aps, out, tokens_per_batch=T, experts=E, rank=R, adapters=NA)
    r = run_bass_kernel_spmd(nc, [arrays], core_ids=[0])
    return r.results[0]["out_t"].transpose(1, 3, 2, 0).reshape(B, T, D)
```

```python
from contextlib import ExitStack

import concourse.bass as bass
from concourse import mybir

P = 128
F32 = mybir.dt.float32
F32R = mybir.dt.float32r
BF16 = mybir.dt.bfloat16
I32 = mybir.dt.int32
U32 = mybir.dt.uint32
ALU = mybir.AluOpType
ACT = mybir.ActivationFunctionType

LANG_BIAS = 5.0
SCALING0 = 32.0 / 16.0
WARM = 10


def two_block_kernel(nc, x, adapter_id, language_id, w, aw, b0, table, out, *, tokens_per_batch, experts,
                     rank, adapters):
    _, NB, K, TB = x.shape
    D = K * P
    AWN = aw.shape[2]
    H = experts * rank
    TILES = TB // P
    BPG = P // rank
    GT = BPG * tokens_per_batch
    GPB = TB // GT
    NG = NB * GPB
    assert H == P and GPB == 2 and K == 4 and TILES == 4 and 2 * AWN <= 512
    SLOTS = 2 * GPB

    with ExitStack() as ctx:
        def sb(name, shape, dt=F32):
            return ctx.enter_context(nc.sbuf_tensor(name, shape, dt))

        def psum(name):
            return ctx.enter_context(nc.psum_tensor(name, [P, 512], F32))

        def sem(name):
            return ctx.enter_context(nc.semaphore(name))

        xs = sb("xs", [P, NB, K, TB])
        x_hi, x_lo = sb("x_hi", [P, 2, K, TB], F32R), sb("x_lo", [P, 2, K, TB], F32R)
        x1_hi, x1_lo = sb("x1_hi", [P, K, TB], F32R), sb("x1_lo", [P, K, TB], F32R)
        ws = sb("ws", [P, K, K, P])
        w_hi, w_lo = sb("w_hi", [P, K, K, P], F32R), sb("w_lo", [P, K, K, P], F32R)
        aws = sb("aws", [P, K, AWN])
        aw_hl = sb("aw_hl", [P, K, 2, AWN], F32R)
        b0s = sb("b0s", [P, D])
        b0_hi, b0_lo = sb("b0_hi", [P, D], F32R), sb("b0_lo", [P, D], F32R)
        rows = sb("rows", [P, SLOTS, 2, D])
        a1_hi, a1_lo = sb("a1_hi", [P, SLOTS, D], F32R), sb("a1_lo", [P, SLOTS, D], F32R)
        bt_hi, bt_lo = sb("bt_hi", [P, GPB, K, P], F32R), sb("bt_lo", [P, GPB, K, P], F32R)
        aw_rest = sb("aw_rest", [P, 2, AWN])
        hw = sb("hw", [P, TILES, AWN])
        logits = sb("logits", [P, TILES, experts])
        top = sb("top", [P, TILES, 8])
        top_at = sb("top_at", [P, TILES, 8], U32)
        gap = sb("gap", [P, TILES])
        gap_exp = sb("gap_exp", [P, TILES])
        denom = sb("denom", [P, TILES])
        inv = sb("inv", [P, TILES])
        weight = sb("weight", [P, TILES, 2])
        picked = sb("picked", [P, TILES, 2, experts])
        picked_w = sb("picked_w", [P, TILES, 2, experts])
        gate = sb("gate", [P, TILES, experts])
        gated = sb("gated", [P, TILES, H])
        gt_hi, gt_lo = sb("gt_hi", [P, TB], F32R), sb("gt_lo", [P, TB], F32R)
        down = sb("down", [P, GPB, GT])
        down_hi, down_lo = sb("down_hi", [P, GPB, GT], F32R), sb("down_lo", [P, GPB, GT], F32R)
        zeros = sb("zeros", [P, 512], BF16)
        table_warm = sb("table_warm", [P, 1])
        ident = sb("ident", [P, P])
        own_batch = sb("own_batch", [P, BPG])
        expert_no = sb("expert_no", [P, experts])
        part_no = sb("part_no", [P, 1], I32)
        rank_no = sb("rank_no", [P, 1], I32)
        adapter_ids = sb("adapter_ids", [P, NG], I32)
        wrap = sb("wrap", [P, NG], I32)
        wrapped = sb("wrapped", [P, NG], I32)
        clamped = sb("clamped", [P, NG], I32)
        row_at = sb("row_at", [P, NG], I32)
        language_ids = sb("language_ids", [P, NB, TILES], I32)
        is_language = sb("is_language", [P, NB, TILES, experts])
        bias = sb("bias", [P, NB, TILES, experts])

        main = [psum(f"main{i}") for i in range(4)]
        aw_ps = [psum(f"aw_ps{i}") for i in range(2)]
        side = [psum(f"side{i}") for i in range(2)]

        adapter_loaded, language_loaded = sem("adapter_loaded"), sem("language_loaded")
        x0_loaded = [sem(f"x0_loaded{c}") for c in range(K)]
        x_loaded = [None] + [sem(f"x_loaded{t}") for t in range(1, NB)]
        w_loaded = [sem(f"w_loaded{c}") for c in range(K)]
        aw_loaded, b0_loaded = sem("aw_loaded"), sem("b0_loaded")
        rows_loaded = [sem(f"rows_loaded{g}") for g in range(NG)]
        stored = sem("stored")
        const_step, const_ready = sem("const_step"), sem("const_ready")
        x_lo_ready, a1_lo_ready, w_lo_ready = sem("x_lo_ready"), sem("a1_lo_ready"), sem("w_lo_ready")
        w_hi_ready, aw_hi_ready, b0_hi_ready = sem("w_hi_ready"), sem("aw_hi_ready"), sem("b0_hi_ready")
        x_hi_ready, a1_hi_ready, x1_hi_ready = sem("x_hi_ready"), sem("a1_hi_ready"), sem("x1_hi_ready")
        bt_hi_ready, gt_hi_ready, down_hi_ready = sem("bt_hi_ready"), sem("gt_hi_ready"), sem("down_hi_ready")
        rest_ready, exp_ready = sem("rest_ready"), sem("exp_ready")
        zeros_ready, w0_hi_ready, w0_lo_ready = sem("zeros_ready"), sem("w0_hi_ready"), sem("w0_lo_ready")
        aw_lo_ready, b0_lo_ready = sem("aw_lo_ready"), sem("b0_lo_ready")
        x0_lo_ready, x1_ready, x1_lo_ready = sem("x0_lo_ready"), sem("x1_ready"), sem("x1_lo_ready")
        bt_lo_ready, gt_lo_ready = sem("bt_lo_ready"), sem("gt_lo_ready")
        down_ready, down_lo_ready = sem("down_ready"), sem("down_lo_ready")
        hw_ready, gap_ready, gated_ready = sem("hw_ready"), sem("gap_ready"), sem("gated_ready")
        x2_ready, row_at_ready = sem("x2_ready"), sem("row_at_ready")
        vector_step = sem("vector_step")
        aw_done, base_done, lora_done = sem("aw_done"), sem("base_done"), sem("lora_done")
        gt_done, bt_done, down_done, up_done = sem("gt_done"), sem("bt_done"), sem("down_done"), sem("up_done")

        up_bank = [main[1:] + side[:1]] * (NB - 2) + [main]

        last_banks = main + aw_ps + side

        block = ctx.enter_context(nc.Block())

        @block.sync
        def _(sp):
            sp.dma_start(adapter_ids[:], adapter_id).then_inc(adapter_loaded, 16)
            for c in range(K):
                sp.dma_start(xs[:, 0, c, :], x[:, 0, c, :]).then_inc(x0_loaded[c], 16)
            sp.dma_start(aws[:], aw).then_inc(aw_loaded, 16)
            sp.dma_start(ws[:, 1], w[:, 1]).then_inc(w_loaded[1], 16)
            sp.dma_start(language_ids[:], language_id.rearrange("p (t j) -> p t j", t=NB)).then_inc(language_loaded, 16)
            sp.dma_start(ws[:, 2], w[:, 2]).then_inc(w_loaded[2], 16)
            sp.dma_start(b0s[:], b0).then_inc(b0_loaded, 16)
            sp.dma_start(ws[:, 3], w[:, 3]).then_inc(w_loaded[3], 16)
            sp.wait_ge(x_hi_ready, K)
            sp.dma_start(xs[:, 1], x[:, 1]).then_inc(x_loaded[1], 16)
            for t in range(2, NB):
                sp.wait_ge(base_done, t)
                sp.dma_start(xs[:, t], x[:, t]).then_inc(x_loaded[t], 16)
            for t in range(NB - 1):
                for c in range(K):
                    sp.wait_ge(x2_ready, t * K + c + 1)
                    sp.dma_start(out[:, t, c, :], xs[:, t, c, :]).then_inc(stored, 16)
            for i in range(GPB * K):
                g, c = divmod(i, K)
                n = slice(g * GT, (g + 1) * GT)
                sp.wait_ge(x2_ready, (NB - 1) * K + i + 1)
                sp.dma_start(out[:, NB - 1, c, n], xs[:, NB - 1, c, n]).then_inc(stored, 16)
            sp.wait_ge(stored, 16 * (K * (NB - 1) + GPB * K))

        @block.gpsimd
        def _(pool):
            nc.gpsimd.iota(part_no[:], [[0, 1]], base=0, channel_multiplier=1).then_inc(const_ready, 1)
            nc.gpsimd.iota(expert_no[:], [[1, experts]], base=0, channel_multiplier=0,
                           allow_small_or_imprecise_dtypes=True).then_inc(const_ready, 1)
            nc.gpsimd.memset(ident[:], 0.0).then_inc(const_step, 1)
            nc.gpsimd.memset(own_batch[:], 1.0).then_inc(const_step, 1)
            pool.wait_ge(const_step, 2)
            nc.gpsimd.affine_select(out=ident[:], in_=ident[:], compare_op=ALU.not_equal, fill=1.0, base=0,
                                    pattern=[[-1, P]], channel_multiplier=1).then_inc(const_ready, 1)
            nc.gpsimd.affine_select(out=own_batch[:], in_=own_batch[:], compare_op=ALU.is_ge, fill=0.0, base=0,
                                    pattern=[[-rank, BPG]], channel_multiplier=1).then_inc(const_step, 1)
            pool.wait_ge(const_step, 3)
            nc.gpsimd.affine_select(out=own_batch[:], in_=own_batch[:], compare_op=ALU.is_ge, fill=0.0,
                                    base=rank - 1, pattern=[[rank, BPG]],
                                    channel_multiplier=-1).then_inc(const_ready, 1)

            def gather(g):
                if g >= SLOTS:
                    pool.wait_ge(a1_hi_ready, g - SLOTS + 1)
                    pool.wait_ge(a1_lo_ready, g - SLOTS + 1)
                    pool.wait_ge(bt_done, g - SLOTS + 1)
                nc.gpsimd.indirect_dma_start(
                    rows[:, g % SLOTS].rearrange("p a d -> p (a d)"), None, table,
                    bass.IndirectOffsetOnAxis(ap=row_at[:, g:g + 1], axis=0)).then_inc(rows_loaded[g], 16)

            def split_a1(g):
                pool.wait_ge(a1_hi_ready, g + 1)
                if g >= SLOTS:
                    pool.wait_ge(up_done, K * (g // GPB - 1))
                s = g % SLOTS
                nc.gpsimd.tensor_tensor(a1_lo[:, s], rows[:, s, 1], a1_hi[:, s].bitcast(F32),
                                        ALU.subtract).then_inc(a1_lo_ready, 1)

            pool.wait_ge(row_at_ready, 1)
            pool.wait_ge(x_hi_ready, 1)
            for g in range(GPB):
                gather(g)
            for c in range(1, K):
                pool.wait_ge(w_hi_ready, c)
                nc.gpsimd.tensor_tensor(w_lo[:, c], ws[:, c], w_hi[:, c].bitcast(F32),
                                        ALU.subtract).then_inc(w_lo_ready, 1)
            for t in range(1, NB + 1):
                if t < NB:
                    for c in range(K):
                        pool.wait_ge(x_hi_ready, t * K + c + 1)
                        if t >= 2 and c == 0:
                            pool.wait_ge(base_done, (t - 1) * K)
                        nc.gpsimd.tensor_tensor(x_lo[:, t % 2, c], xs[:, t, c], x_hi[:, t % 2, c].bitcast(F32),
                                                ALU.subtract).then_inc(x_lo_ready, 1)
                if t == 1:
                    for g in range(GPB, SLOTS):
                        gather(g)
                for g in range((t - 1) * GPB, t * GPB):
                    split_a1(g)
                    if g >= 1 and g - 1 + SLOTS < NG:
                        gather(g - 1 + SLOTS)

        @block.scalar
        def _(act):
            act.dma_start(ws[:, 0], w[:, 0]).then_inc(w_loaded[0], 16)
            act.wait_ge(zeros_ready, 1)
            nc.scalar.activation(table_warm[:], zeros[:, 0:1], ACT.Exp)

            def round_hi(dst, src, ready):
                nc.scalar.activation(dst, src, ACT.Copy).then_inc(ready, 1)

            def w_half(c):
                act.wait_ge(w_loaded[c], 16)
                round_hi(w_hi[:, c], ws[:, c], w_hi_ready)

            def x_half(t, c):
                if t == 0:
                    act.wait_ge(x0_loaded[c], 16)
                elif c == 0:
                    act.wait_ge(x_loaded[t], 16)
                    if t >= 2:
                        act.wait_ge(base_done, (t - 1) * K)
                round_hi(x_hi[:, t % 2, c], xs[:, t, c], x_hi_ready)

            def a1_half(g):
                act.wait_ge(rows_loaded[g], 16)
                if g >= SLOTS:
                    act.wait_ge(up_done, K * (g // GPB - 1))
                round_hi(a1_hi[:, g % SLOTS], rows[:, g % SLOTS, 1], a1_hi_ready)

            def copy_rest(u, j):
                n = u * TILES + j
                act.wait_ge(aw_done, n + 1)
                if n >= 2:
                    act.wait_ge(hw_ready, n - 1)
                nc.scalar.activation(aw_rest[:, n % 2], aw_ps[n % 2][:, AWN:2 * AWN], ACT.Copy).then_inc(rest_ready, 1)

            def exp_gap(u):
                act.wait_ge(gap_ready, u + 1)
                nc.scalar.activation(gap_exp[:], gap[:], ACT.Exp).then_inc(exp_ready, 1)

            def gt_half(u):
                act.wait_ge(gt_done, u + 1)
                if u >= 1:
                    act.wait_ge(lora_done, u * K)
                round_hi(gt_hi[:], side[1][:], gt_hi_ready)

            def bt_half(g):
                act.wait_ge(bt_done, g + 1)
                if g >= GPB:
                    act.wait_ge(down_done, g - GPB + 1)
                round_hi(bt_hi[:, g % GPB].rearrange("p k m -> p (k m)"), side[g % 2][:], bt_hi_ready)

            def x1_half(t, c):
                act.wait_ge(x1_ready, t * K + c + 1)
                if t >= 1:
                    act.wait_ge(down_done, t * GPB)
                round_hi(x1_hi[:, c], xs[:, t, c], x1_hi_ready)

            def down_half(g):
                act.wait_ge(down_ready, g + 1)
                if g >= GPB:
                    act.wait_ge(up_done, K * (g // GPB))
                round_hi(down_hi[:, g % GPB], down[:, g % GPB], down_hi_ready)

            for c in range(K):
                x_half(0, c)
            act.wait_ge(aw_loaded, 16)
            round_hi(aw_hl[:, :, 0], aws[:], aw_hi_ready)
            for c in range(1, K):
                w_half(c)
            for j in range(TILES):
                copy_rest(0, j)
            act.wait_ge(b0_loaded, 16)
            round_hi(b0_hi[:], b0s[:], b0_hi_ready)
            exp_gap(0)
            gt_half(0)
            for c in range(K):
                x_half(1, c)
            for c in range(K):
                x1_half(0, c)
            for g in range(GPB):
                bt_half(g)
            for g in range(GPB):
                a1_half(g)
            for t in range(NB):
                more = t + 1 < NB
                if more:
                    for j in range(TILES):
                        copy_rest(t + 1, j)
                    exp_gap(t + 1)
                for g in range(t * GPB, (t + 1) * GPB):
                    down_half(g)
                if more:
                    gt_half(t + 1)
                    a1_half((t + 1) * GPB)
                    if t + 2 < NB:
                        for c in range(K):
                            x_half(t + 2, c)
                    x1_half(t + 1, 0)
                    a1_half((t + 1) * GPB + 1)
                    x1_half(t + 1, 1)
                    bt_half((t + 1) * GPB)
                    x1_half(t + 1, 2)
                    bt_half((t + 1) * GPB + 1)
                    x1_half(t + 1, 3)

        @block.vector
        def _(dve):
            steps = [0]

            def then_wait(instruction):
                steps[0] += 1
                instruction.then_inc(vector_step, 1)
                dve.wait_ge(vector_step, steps[0])

            def split_lo(dst, src, hi, ready):
                nc.vector.tensor_tensor(dst, src, hi.bitcast(F32), ALU.subtract).then_inc(ready, 1)

            def add_rest(u, j):
                n = u * TILES + j
                dve.wait_ge(rest_ready, n + 1)
                nc.vector.tensor_tensor(hw[:, j], aw_ps[n % 2][:, 0:AWN], aw_rest[:, n % 2],
                                        ALU.add).then_inc(hw_ready, 1)

            def top_two(u):
                dve.wait_ge(hw_ready, (u + 1) * TILES)
                then_wait(nc.vector.tensor_tensor(logits[:], hw[:, :, H:AWN], bias[:, u], ALU.add))
                for j in range(TILES):
                    last = nc.vector.max(top[:, j], logits[:, j])
                then_wait(last)
                nc.vector.tensor_tensor(gap[:], top[:, :, 1], top[:, :, 0], ALU.subtract).then_inc(gap_ready, 1)
                for j in range(TILES):
                    last = nc.vector.max_index(top_at[:, j], top[:, j], logits[:, j])
                then_wait(last)

            def gate_h(u):
                dve.wait_ge(exp_ready, u + 1)
                then_wait(nc.vector.tensor_scalar(denom[:], gap_exp[:], 1.0, None, ALU.add))
                then_wait(nc.vector.reciprocal(inv[:], denom[:]))
                nc.vector.tensor_scalar(weight[:, :, 0], inv[:], SCALING0, None, ALU.mult)
                then_wait(nc.vector.scalar_tensor_tensor(weight[:, :, 1], gap_exp[:], SCALING0, inv[:],
                                                         ALU.mult, ALU.mult))
                then_wait(nc.vector.tensor_tensor(
                    picked_w[:], picked[:], weight[:].unsqueeze(3).broadcast_to([P, TILES, 2, experts]), ALU.mult))
                then_wait(nc.vector.tensor_tensor(gate[:], picked_w[:, :, 0], picked_w[:, :, 1], ALU.add))
                if u >= 1:
                    dve.wait_ge(gt_done, u)
                nc.vector.tensor_tensor(
                    gated[:].rearrange("p j (e r) -> p j e r", e=experts),
                    hw[:, :, 0:H].rearrange("p j (e r) -> p j e r", e=experts),
                    gate[:].unsqueeze(3).broadcast_to([P, TILES, experts, rank]), ALU.mult).then_inc(gated_ready, 1)

            def pick():
                then_wait(nc.vector.tensor_tensor(
                    picked[:], top_at[:, :, 0:2].unsqueeze(3).broadcast_to([P, TILES, 2, experts]),
                    expert_no[:].unsqueeze(1).unsqueeze(1).broadcast_to([P, TILES, 2, experts]), ALU.is_equal))

            def add_x1(t, c):
                dve.wait_ge(lora_done, t * K + c + 1)
                nc.vector.tensor_tensor(xs[:, t, c], main[c][:], xs[:, t, c], ALU.add).then_inc(x1_ready, 1)

            def x1_rest(t, c):
                dve.wait_ge(x1_hi_ready, t * K + c + 1)
                split_lo(x1_lo[:, c], xs[:, t, c], x1_hi[:, c], x1_lo_ready)

            def mask_down(g):
                dve.wait_ge(down_done, g + 1)
                nc.vector.tensor_tensor(
                    down[:, g % GPB].rearrange("p (b n) -> p b n", b=BPG),
                    side[g % 2][:, 0:GT].rearrange("p (b n) -> p b n", b=BPG),
                    own_batch[:].unsqueeze(2).broadcast_to([P, BPG, tokens_per_batch]),
                    ALU.mult).then_inc(down_ready, 1)

            def down_rest(g):
                dve.wait_ge(down_hi_ready, g + 1)
                split_lo(down_lo[:, g % GPB], down[:, g % GPB], down_hi[:, g % GPB], down_lo_ready)

            def gt_rest(u):
                dve.wait_ge(gt_hi_ready, u + 1)
                split_lo(gt_lo[:], side[1][:], gt_hi[:], gt_lo_ready)

            def bt_rest(g):
                dve.wait_ge(bt_hi_ready, g + 1)
                split_lo(bt_lo[:, g % GPB].rearrange("p k m -> p (k m)"), side[g % 2][:],
                         bt_hi[:, g % GPB].rearrange("p k m -> p (k m)"), bt_lo_ready)

            def add_x2_last(s, c):
                n = slice(s * GT, (s + 1) * GT)
                dve.wait_ge(up_done, (NB - 1) * K + s * K + c + 1)
                nc.vector.tensor_tensor(xs[:, NB - 1, c, n], last_banks[s * K + c][:, 0:GT], xs[:, NB - 1, c, n],
                                        ALU.add).then_inc(x2_ready, 1)

            def add_x2(t, c):
                dve.wait_ge(up_done, t * K + c + 1)
                nc.vector.tensor_tensor(xs[:, t, c], up_bank[t][c][:], xs[:, t, c],
                                        ALU.add).then_inc(x2_ready, 1)

            nc.vector.memset(zeros[:], 0.0).then_inc(zeros_ready, 1)
            dve.wait_ge(const_ready, 2)
            dve.wait_ge(adapter_loaded, 16)
            then_wait(nc.vector.tensor_scalar(rank_no[:], part_no[:], rank - 1, None, ALU.bitwise_and))
            then_wait(nc.vector.tensor_scalar(wrap[:], adapter_ids[:], 0.0, float(adapters), ALU.is_lt, ALU.mult))
            then_wait(nc.vector.tensor_tensor(wrapped[:], wrap[:], adapter_ids[:], ALU.add))
            then_wait(nc.vector.tensor_scalar(clamped[:], wrapped[:], 0.0, float(adapters - 1), ALU.max, ALU.min))
            nc.vector.scalar_tensor_tensor(row_at[:], clamped[:], float(rank), rank_no[:].broadcast_to([P, NG]),
                                           ALU.mult, ALU.add).then_inc(row_at_ready, 1)
            dve.wait_ge(w_loaded[0], 16)
            nc.vector.tensor_copy(w_hi[:, 0], ws[:, 0]).then_inc(w0_hi_ready, 1)
            dve.wait_ge(w0_hi_ready, 1)
            split_lo(w_lo[:, 0], ws[:, 0], w_hi[:, 0], w0_lo_ready)
            for c in range(K):
                dve.wait_ge(x_hi_ready, c + 1)
                split_lo(x_lo[:, 0, c], xs[:, 0, c], x_hi[:, 0, c], x0_lo_ready)
            dve.wait_ge(aw_hi_ready, 1)
            split_lo(aw_hl[:, :, 1], aws[:], aw_hl[:, :, 0], aw_lo_ready)
            dve.wait_ge(language_loaded, 16)
            then_wait(nc.vector.tensor_tensor(
                is_language[:].rearrange("p t j e -> p (t j) e"),
                language_ids[:].rearrange("p t j -> p (t j)").unsqueeze(2).broadcast_to([P, NB * TILES, experts]),
                expert_no[:].unsqueeze(1).broadcast_to([P, NB * TILES, experts]), ALU.is_equal))
            then_wait(nc.vector.tensor_scalar(bias[:], is_language[:], LANG_BIAS, None, ALU.mult))
            for j in range(TILES):
                add_rest(0, j)
            dve.wait_ge(b0_hi_ready, 1)
            split_lo(b0_lo[:], b0s[:], b0_hi[:], b0_lo_ready)
            top_two(0)
            pick()
            gate_h(0)
            gt_rest(0)
            dve.wait_ge(const_ready, 4)
            add_x1(0, 0)
            for c in range(1, K):
                add_x1(0, c)
                x1_rest(0, c - 1)
            for g in range(GPB):
                bt_rest(g)
            for t in range(NB):
                more = t + 1 < NB
                if more:
                    for j in range(TILES):
                        add_rest(t + 1, j)
                        if j == 0:
                            x1_rest(t, K - 1)
                    top_two(t + 1)
                    pick()
                    gate_h(t + 1)
                groups = range(t * GPB, (t + 1) * GPB)
                for g in groups:
                    mask_down(g)
                    if not more:
                        down_rest(g)
                if more:
                    for g in groups:
                        down_rest(g)
                if more:
                    gt_rest(t + 1)
                    if t < NB - 2:
                        for c in range(K):
                            add_x2(t, c)
                    for c in range(K):
                        add_x1(t + 1, c)
                        if c < K - 1:
                            x1_rest(t + 1, c)
                        if 1 <= c <= GPB:
                            bt_rest((t + 1) * GPB + c - 1)
                    if t == NB - 2:
                        x1_rest(t + 1, K - 1)
                        for c in range(K):
                            add_x2(t, c)
                else:
                    for i in range(GPB * K):
                        add_x2_last(*divmod(i, K))

        @block.tensor
        def _(pe):
            def three(out_ap, terms):
                for i, (lhsT, rhs) in enumerate(terms):
                    last = nc.tensor.matmul(out_ap, lhsT, rhs, start=(i == 0), stop=(i == len(terms) - 1))
                return last

            def base(t, c):
                s = t % 2
                if c == 0:
                    pe.wait_ge(w0_hi_ready, 1)
                else:
                    pe.wait_ge(w_hi_ready, c)
                if t >= 1:
                    if c == 0:
                        pe.wait_ge(x1_ready, (t - 1) * K + 1)
                    elif t == NB - 1:
                        pe.wait_ge(x1_ready, (t - 1) * K + c + 1)
                    else:
                        pe.wait_ge(x2_ready, (t - 1) * K + c)
                for k in range(K):
                    if t == 0 and c == 0:
                        pe.wait_ge(x_hi_ready, k + 1)
                    nc.tensor.matmul(main[c][:], w_hi[:, c, k], x_hi[:, s, k], start=(k == 0), stop=False)
                if c == 0:
                    pe.wait_ge(w0_lo_ready, 1)
                else:
                    pe.wait_ge(w_lo_ready, c)
                for k in range(K):
                    nc.tensor.matmul(main[c][:], w_lo[:, c, k], x_hi[:, s, k], start=False, stop=False)
                for k in range(K):
                    if t == 0 and c == 0:
                        pe.wait_ge(x0_lo_ready, k + 1)
                    last = nc.tensor.matmul(main[c][:], w_hi[:, c, k], x_lo[:, s, k], start=False, stop=False)
                last.then_inc(base_done, 1)

            def lora(t, c):
                if c == 0:
                    pe.wait_ge(gt_hi_ready, t + 1)
                    pe.wait_ge(gt_lo_ready, t + 1)
                    pe.wait_ge(b0_hi_ready, 1)
                    pe.wait_ge(b0_lo_ready, 1)
                m = slice(c * P, (c + 1) * P)
                nc.tensor.matmul(main[c][:], b0_hi[:, m], gt_hi[:], start=False, stop=False)
                nc.tensor.matmul(main[c][:], b0_lo[:, m], gt_hi[:], start=False, stop=False)
                nc.tensor.matmul(main[c][:], b0_hi[:, m], gt_lo[:], start=False, stop=True).then_inc(lora_done, 1)

            def aw_tiles(u):
                s = u % 2
                pe.wait_ge(aw_hi_ready, 1)
                pe.wait_ge(aw_lo_ready, 1)
                if u >= 1:
                    pe.wait_ge(x_hi_ready, (u + 1) * K)
                    pe.wait_ge(x_lo_ready, u * K)
                for j in range(TILES):
                    n = u * TILES + j
                    if n >= 2:
                        pe.wait_ge(hw_ready, n - 1)
                    m = slice(j * P, (j + 1) * P)
                    for k in range(K):
                        nc.tensor.matmul(aw_ps[n % 2][:, 0:2 * AWN], x_hi[:, s, k, m],
                                         aw_hl[:, k].rearrange("p h n -> p (h n)"), start=(k == 0), stop=False)
                        last = nc.tensor.matmul(aw_ps[n % 2][:, 0:AWN], x_lo[:, s, k, m], aw_hl[:, k, 0],
                                                start=False, stop=(k == K - 1))
                    last.then_inc(aw_done, 1)

            def gt_transposes(u):
                pe.wait_ge(gated_ready, u + 1)
                if u == 0:
                    pe.wait_ge(const_ready, 3)
                else:
                    pe.wait_ge(down_ready, u * GPB)
                for j in range(TILES):
                    last = nc.tensor.transpose(side[1][:, j * P:(j + 1) * P], gated[:, j], ident[:])
                last.then_inc(gt_done, 1)

            def bt_transposes(g):
                pe.wait_ge(rows_loaded[g], 16)
                if g % 2 == 1:
                    pe.wait_ge(gt_lo_ready, g // 2 + 1)
                elif g == (NB - 1) * GPB:
                    pe.wait_ge(down_ready, g - 1)
                elif g >= GPB:
                    pe.wait_ge(x2_ready, g // GPB * K)
                for k in range(K):
                    last = nc.tensor.transpose(side[g % 2][:, k * P:(k + 1) * P],
                                               rows[:, g % SLOTS, 0, k * P:(k + 1) * P], ident[:])
                last.then_inc(bt_done, 1)

            def down_group(g):
                t, s = g // GPB, g % GPB
                n = slice(s * GT, (s + 1) * GT)
                pe.wait_ge(bt_hi_ready, g + 1)
                pe.wait_ge(bt_lo_ready, g + 1)
                terms = []
                for k in range(K):
                    terms += [(bt_hi[:, s, k], x1_hi[:, k, n]), (bt_lo[:, s, k], x1_hi[:, k, n]),
                              (bt_hi[:, s, k], x1_lo[:, k, n])]
                pe.wait_ge(x1_hi_ready, (t + 1) * K)
                pe.wait_ge(x1_lo_ready, (t + 1) * K)
                three(side[g % 2][:, 0:GT], terms).then_inc(down_done, 1)

            def up(t, c):
                bank = up_bank[t][c]
                if t == NB - 2:
                    pe.wait_ge(x1_ready, (t + 1) * K + c + 1)
                elif c < K - 1:
                    pe.wait_ge(x1_ready, t * K + c + 2)
                m = slice(c * P, (c + 1) * P)
                for g in range(t * GPB, (t + 1) * GPB):
                    s, a = g % GPB, g % SLOTS
                    if c == 0:
                        pe.wait_ge(a1_lo_ready, g + 1)
                        pe.wait_ge(down_lo_ready, g + 1)
                    last = three(bank[:, s * GT:(s + 1) * GT],
                                 [(a1_hi[:, a, m], down_hi[:, s]), (a1_lo[:, a, m], down_hi[:, s]),
                                  (a1_hi[:, a, m], down_lo[:, s])])
                last.then_inc(up_done, 1)

            def up_last(s, c):
                g, m = (NB - 1) * GPB + s, slice(c * P, (c + 1) * P)
                if c == 0:
                    pe.wait_ge(a1_lo_ready, g + 1)
                    pe.wait_ge(down_lo_ready, g + 1)
                    pe.wait_ge(x2_ready, (NB - 1) * K)
                three(last_banks[s * K + c][:, 0:GT],
                      [(a1_hi[:, g % SLOTS, m], down_hi[:, s]), (a1_lo[:, g % SLOTS, m], down_hi[:, s]),
                       (a1_hi[:, g % SLOTS, m], down_lo[:, s])]).then_inc(up_done, 1)

            pe.wait_ge(zeros_ready, 1)
            for _ in range(WARM):
                nc.tensor.matmul(side[0][:], zeros[:, 0:P], zeros[:], start=True, stop=True)
            base(0, 0)
            aw_tiles(0)
            base(0, 1)
            base(0, 2)
            gt_transposes(0)
            base(0, 3)
            for c in range(K):
                lora(0, c)
            for g in range(GPB):
                bt_transposes(g)
            for t in range(NB - 1):
                aw_tiles(t + 1)
                for g in range(t * GPB, (t + 1) * GPB):
                    down_group(g)
                base(t + 1, 0)
                gt_transposes(t + 1)
                if t < NB - 2:
                    for c in range(K):
                        up(t, c)
                    lora(t + 1, 0)
                base(t + 1, 1)
                if t == NB - 2:
                    lora(t + 1, 0)
                for c in range(1, K):
                    if c > 1:
                        base(t + 1, c)
                    lora(t + 1, c)
                    if c <= GPB:
                        bt_transposes((t + 1) * GPB + c - 1)
            for c in range(K):
                up(NB - 2, c)
            for g in range((NB - 1) * GPB, NG):
                down_group(g)
            for i in range(GPB * K):
                up_last(*divmod(i, K))


def kernel(x, itok_B_0_7, itok_B_4_50, L0_cond_W, L0_cond_Wr, L0_cond_A, L0_cond_B, L1_cond_A, L1_cond_B):
    import numpy as np
    import concourse.bacc as bacc
    from concourse.bass_utils import run_bass_kernel_spmd

    x, w, wr, a0, b0, a1, b1 = (np.asarray(v) for v in (
        x, L0_cond_W, L0_cond_Wr, L0_cond_A, L0_cond_B, L1_cond_A, L1_cond_B))
    adapter, language = np.asarray(itok_B_4_50), np.asarray(itok_B_0_7)
    B, T, D = x.shape
    E, R, _ = a0.shape
    NA = a1.shape[0]
    K, TB = D // P, 512
    NB = B * T // TB
    arrays = {
        "x_t": x.reshape(NB, TB, K, P).transpose(3, 0, 2, 1),
        "adapter_id": np.repeat(adapter.reshape(-1, P // R).T, R, axis=0),
        "language_id": np.repeat(language.reshape(-1, P // T).T, T, axis=0),
        "w_t": w.reshape(K, P, K, P).transpose(3, 0, 2, 1),
        "aw_t": np.concatenate([a0.reshape(E * R, D), wr]).T.reshape(K, P, -1).transpose(1, 0, 2),
        "b0_t": b0.transpose(0, 2, 1).reshape(E * R, D),
        "table": np.concatenate([b1.reshape(NA * R, D), a1.transpose(0, 2, 1).reshape(NA * R, D)], axis=1),
    }
    arrays = {k: np.ascontiguousarray(v) for k, v in arrays.items()}

    nc = bacc.Bacc("TRN2", target_bir_lowering=False, num_devices=1)
    aps = [nc.dram_tensor(k, v.shape, mybir.dt.from_np(v.dtype), kind="ExternalInput").ap() for k, v in arrays.items()]
    out = nc.dram_tensor("out_t", arrays["x_t"].shape, F32, kind="ExternalOutput").ap()
    two_block_kernel(nc, *aps, out, tokens_per_batch=T, experts=E, rank=R, adapters=NA)
    r = run_bass_kernel_spmd(nc, [arrays], core_ids=[0])
    return r.results[0]["out_t"].transpose(1, 3, 2, 0).reshape(B, T, D)
```

```python
from contextlib import ExitStack

import concourse.bass as bass
from concourse import mybir

P = 128
F32 = mybir.dt.float32
F32R = mybir.dt.float32r
BF16 = mybir.dt.bfloat16
I32 = mybir.dt.int32
U32 = mybir.dt.uint32
ALU = mybir.AluOpType
ACT = mybir.ActivationFunctionType

LANG_BIAS = 5.0
SCALING0 = 32.0 / 16.0
WARM = 6


def two_block_kernel(nc, x, adapter_id, adapter_list, language_id, w, aw, b0, a1, b1, out, *, tokens_per_batch,
                     experts, rank, adapters):
    _, NB, K, TB = x.shape
    D = K * P
    AWN = aw.shape[2]
    H = experts * rank
    TILES = TB // P
    BPG = P // rank
    GT = BPG * tokens_per_batch
    GPB = TB // GT
    NG = NB * GPB
    CW = 32
    CT = P // CW
    BPT = CW // rank
    NT = BPT * tokens_per_batch
    assert H == P and GPB == 2 and K == 4 and TILES == 4 and TILES // 2 * AWN <= 512
    SLOTS = 2 * GPB

    with ExitStack() as ctx:
        def sb(name, shape, dt=F32):
            return ctx.enter_context(nc.sbuf_tensor(name, shape, dt))

        def psum(name):
            return ctx.enter_context(nc.psum_tensor(name, [P, 512], F32))

        def sem(name):
            return ctx.enter_context(nc.semaphore(name))

        xs = sb("xs", [P, NB, K, TB])
        x_hi, x_lo = sb("x_hi", [P, 2, K, TB], F32R), sb("x_lo", [P, 2, K, TB], F32R)
        ws = sb("ws", [P, K, K, P])
        w_hi, w_lo = sb("w_hi", [P, K, K, P], F32R), sb("w_lo", [P, K, K, P], F32R)
        aws = sb("aws", [P, K, AWN])
        b0s = sb("b0s", [P, D])
        b0_hi, b0_lo = sb("b0_hi", [P, D], F32R), sb("b0_lo", [P, D], F32R)
        rows = sb("rows", [P, SLOTS, D])
        b1s = sb("b1s", [P, NG, BPG * rank, K])
        a1_ops = sb("a1_ops", [P, SLOTS, 2, D], F32R)
        a1_hi, a1_rest = sb("a1_hi", [P, GPB, D], F32R), sb("a1_rest", [P, GPB, D])
        logits = sb("logits", [P, TILES, experts])
        top = sb("top", [P, TILES, 8])
        top_at = sb("top_at", [P, TILES, 8], U32)
        gap = sb("gap", [P, TILES])
        gap_exp = sb("gap_exp", [P, TILES])
        denom = sb("denom", [P, TILES])
        inv = sb("inv", [P, TILES])
        weight = sb("weight", [P, TILES, 2])
        picked = sb("picked", [P, TILES, 2, experts])
        picked_w = sb("picked_w", [P, TILES, 2, experts])
        gate = sb("gate", [P, TILES, experts])
        gated = sb("gated", [P, TILES, H])
        gt_hi, gt_lo = sb("gt_hi", [P, TB], F32R), sb("gt_lo", [P, TB], F32R)
        down = sb("down", [P, GPB, GT])
        down_ops = sb("down_ops", [P, SLOTS, 2, GT], F32R)
        zeros = sb("zeros", [P, 512], BF16)
        table_warm = sb("table_warm", [P, 1])
        ident = sb("ident", [P, P])
        own_batch = sb("own_batch", [P, BPG])
        own_in_half = sb("own_in_half", [P, BPG // 2])
        expert_no = sb("expert_no", [P, experts])
        part_no = sb("part_no", [P, 1], I32)
        rank_no = sb("rank_no", [P, 1], I32)
        adapter_ids = sb("adapter_ids", [P, NG], I32)
        adapter_row = sb("adapter_row", [1, NG * BPG], I32)
        row_wrap = sb("row_wrap", [1, NG * BPG], I32)
        row_wrapped = sb("row_wrapped", [1, NG * BPG], I32)
        row_clamped = sb("row_clamped", [1, NG * BPG], I32)
        wrap = sb("wrap", [P, NG], I32)
        wrapped = sb("wrapped", [P, NG], I32)
        clamped = sb("clamped", [P, NG], I32)
        row_at = sb("row_at", [P, NG], I32)
        language_ids = sb("language_ids", [P, NB, TILES], I32)
        is_language = sb("is_language", [P, NB, TILES, experts])
        bias = sb("bias", [P, NB, TILES, experts])

        main = [psum(f"main{i}") for i in range(4)]
        aw_ps = [psum(f"aw_ps{i}") for i in range(2)]
        side = [psum(f"side{i}") for i in range(2)]

        adapter_loaded, language_loaded = sem("adapter_loaded"), sem("language_loaded")
        x0_loaded = [sem(f"x0_loaded{c}") for c in range(K)]
        x_loaded = [None] + [sem(f"x_loaded{t}") for t in range(1, NB)]
        w_loaded = [sem(f"w_loaded{c}") for c in range(K)]
        aw_loaded = [sem("aw_loaded0"), sem("aw_loaded_rest")]
        b0_loaded = sem("b0_loaded")
        rows_loaded = [sem(f"rows_loaded{g}") for g in range(NG)]
        b1_loaded = [sem(f"b1_loaded{g}") for g in range(NG)]
        stored = sem("stored")
        const_step, const_ready = sem("const_step"), sem("const_ready")
        x_lo_ready, a1_lo_ready, w_lo_ready = sem("x_lo_ready"), sem("a1_lo_ready"), sem("w_lo_ready")
        w_hi_ready, b0_hi_ready = sem("w_hi_ready"), sem("b0_hi_ready")
        x_hi_ready, a1_hi_ready, a1_packed = sem("x_hi_ready"), sem("a1_hi_ready"), sem("a1_packed")
        gt_hi_ready, down_hi_ready = sem("gt_hi_ready"), sem("down_hi_ready")
        exp_ready = sem("exp_ready")
        zeros_ready, w0_hi_ready, w0_lo_ready = sem("zeros_ready"), sem("w0_hi_ready"), sem("w0_lo_ready")
        b0_lo_ready = sem("b0_lo_ready")
        x0_lo_ready, x1_ready = sem("x0_lo_ready"), sem("x1_ready")
        gt_lo_ready = sem("gt_lo_ready")
        down_ready, down_lo_ready = sem("down_ready"), sem("down_lo_ready")
        pads_ready = sem("pads_ready")
        gap_ready, gated_ready = sem("gap_ready"), sem("gated_ready")
        x2_ready, row_at_ready, row_clamped_ready = sem("x2_ready"), sem("row_at_ready"), sem("row_clamped_ready")
        vector_step = sem("vector_step")
        aw_done, base_done, lora_done = sem("aw_done"), sem("base_done"), sem("lora_done")
        gt_done, down_done, up_done = sem("gt_done"), sem("down_done"), sem("up_done")

        PARTS = K * GPB
        up_banks = main[2:] + side[:1] + aw_ps + side[:1] + aw_ps
        EARLY = 5
        last_banks = main + side + aw_ps
        last_x1_banks = [main[K - 1], aw_ps[0]]

        halves = [slice(0, P // 2), slice(P // 2, P)]

        def packed(g):
            return g // GPB < NB - 1

        def h_parts(u):
            if u == 0:
                banks, n = [side[1], side[0]] + aw_ps, 1
            else:
                banks, n = aw_ps, TILES // 2
            return [(slice(i * n, (i + 1) * n), bank[:, 0:n * AWN].rearrange("p (j n) -> p j n", j=n))
                    for i, bank in enumerate(banks)]

        block = ctx.enter_context(nc.Block())

        @block.sync
        def _(sp):
            for c in range(K):
                sp.dma_start(xs[:, 0, c, :], x[:, 0, c, :]).then_inc(x0_loaded[c], 16)
            sp.dma_start(ws[:, 0], w[:, 0]).then_inc(w_loaded[0], 16)
            sp.dma_start(ws[:, 1], w[:, 1]).then_inc(w_loaded[1], 16)
            sp.dma_start(adapter_ids[:], adapter_id).then_inc(adapter_loaded, 16)
            sp.dma_start(adapter_row[:], adapter_list).then_inc(adapter_loaded, 16)
            sp.dma_start(language_ids[:], language_id.rearrange("p (t j) -> p t j", t=NB)).then_inc(language_loaded, 16)
            sp.dma_start(ws[:, 2], w[:, 2]).then_inc(w_loaded[2], 16)
            sp.dma_start(b0s[:], b0).then_inc(b0_loaded, 16)
            sp.dma_start(ws[:, 3], w[:, 3]).then_inc(w_loaded[3], 16)
            sp.dma_start(xs[:, 1], x[:, 1]).then_inc(x_loaded[1], 16)

            def load_b1(g):
                _, ids = nc.values_load_multi_w_load_instructions(
                    row_clamped[0:1, g * BPG:(g + 1) * BPG], engines=[mybir.EngineType.SP], min_val=0,
                    max_val=adapters - 1, skip_runtime_bounds_check_because="VectorE clamped them")
                for b, adapter in enumerate(ids):
                    sp.dma_start(b1s[:, g, b * rank:(b + 1) * rank],
                                 b1[bass.ds(adapter, 1)].rearrange("a p (r k) -> p (a r) k", k=K))\
                      .then_inc(b1_loaded[g], 16)

            sp.wait_ge(row_clamped_ready, 1)
            for t in range(NB):
                for g in range(t * GPB, (t + 1) * GPB):
                    load_b1(g)
                if t + 2 < NB:
                    sp.dma_start(xs[:, t + 2], x[:, t + 2]).then_inc(x_loaded[t + 2], 16)
            for t in range(NB - 1):
                for c in range(K):
                    sp.wait_ge(x2_ready, t * PARTS + (c + 1) * GPB)
                    sp.dma_start(out[:, t, c, :], xs[:, t, c, :]).then_inc(stored, 16)
            for s in range(GPB):
                n = slice(s * GT, (s + 1) * GT)
                for c in range(2, K + 1, 2):
                    sp.wait_ge(x2_ready, (NB - 1) * PARTS + s * K + c)
                    sp.dma_start(out[:, NB - 1, c - 2:c, n], xs[:, NB - 1, c - 2:c, n]).then_inc(stored, 16)
            sp.wait_ge(stored, 16 * (K * (NB - 1) + GPB * K // 2))

        @block.gpsimd
        def _(pool):
            nc.gpsimd.iota(part_no[:], [[0, 1]], base=0, channel_multiplier=1).then_inc(const_ready, 1)
            nc.gpsimd.iota(expert_no[:], [[1, experts]], base=0, channel_multiplier=0,
                           allow_small_or_imprecise_dtypes=True).then_inc(const_ready, 1)
            nc.gpsimd.memset(ident[:], 0.0).then_inc(const_step, 1)
            nc.gpsimd.memset(own_batch[:], 1.0).then_inc(const_step, 1)
            pool.wait_ge(const_step, 2)
            nc.gpsimd.affine_select(out=ident[:], in_=ident[:], compare_op=ALU.not_equal, fill=1.0, base=0,
                                    pattern=[[-1, P]], channel_multiplier=1).then_inc(const_ready, 1)
            nc.gpsimd.affine_select(out=own_batch[:], in_=own_batch[:], compare_op=ALU.is_ge, fill=0.0, base=0,
                                    pattern=[[-rank, BPG]], channel_multiplier=1).then_inc(const_step, 1)
            pool.wait_ge(const_step, 3)
            nc.gpsimd.affine_select(out=own_batch[:], in_=own_batch[:], compare_op=ALU.is_ge, fill=0.0,
                                    base=rank - 1, pattern=[[rank, BPG]],
                                    channel_multiplier=-1).then_inc(const_ready, 1)

            def gather(g):
                if g >= SLOTS:
                    pool.wait_ge(a1_hi_ready, g - SLOTS + 1)
                    pool.wait_ge(a1_lo_ready, g - SLOTS + 1)
                nc.gpsimd.indirect_dma_start(
                    rows[:, g % SLOTS], None, a1,
                    bass.IndirectOffsetOnAxis(ap=row_at[:, g:g + 1], axis=0)).then_inc(rows_loaded[g], 16)

            def split_a1(g):
                pool.wait_ge(a1_hi_ready, g + 1)
                if g >= SLOTS:
                    pool.wait_ge(up_done, PARTS * (g // GPB - 1))
                s = g % SLOTS
                if packed(g):
                    if g >= GPB:
                        pool.wait_ge(a1_packed, g - GPB + 1)
                    hi, lo = a1_hi[:, g % GPB], a1_rest[:, g % GPB]
                else:
                    hi, lo = a1_ops[:, s, 0], a1_ops[:, s, 1]
                nc.gpsimd.tensor_tensor(lo, rows[:, s], hi.bitcast(F32), ALU.subtract).then_inc(a1_lo_ready, 1)

            for c in range(1, K):
                pool.wait_ge(w_hi_ready, c)
                nc.gpsimd.tensor_tensor(w_lo[:, c], ws[:, c], w_hi[:, c].bitcast(F32),
                                        ALU.subtract).then_inc(w_lo_ready, 1)
            pool.wait_ge(row_at_ready, 1)
            for g in range(GPB):
                gather(g)
            for t in range(1, NB + 1):
                if t < NB:
                    for c in range(K):
                        pool.wait_ge(x_hi_ready, t * K + c + 1)
                        if t >= 2 and c == 0:
                            pool.wait_ge(base_done, (t - 1) * K)
                        nc.gpsimd.tensor_tensor(x_lo[:, t % 2, c], xs[:, t, c], x_hi[:, t % 2, c].bitcast(F32),
                                                ALU.subtract).then_inc(x_lo_ready, 1)
                if t == 1:
                    for g in range(GPB, SLOTS):
                        gather(g)
                for g in range((t - 1) * GPB, t * GPB):
                    split_a1(g)
                    if g >= 1 and g - 1 + SLOTS < NG:
                        gather(g - 1 + SLOTS)

        @block.scalar
        def _(act):
            act.dma_start(aws[:, 0], aw[:, 0]).then_inc(aw_loaded[0], 16)
            act.dma_start(aws[:, 1:], aw[:, 1:]).then_inc(aw_loaded[1], 16)
            act.wait_ge(zeros_ready, 1)
            nc.scalar.activation(table_warm[:], zeros[:, 0:1], ACT.Exp)

            def round_hi(dst, src, ready):
                nc.scalar.activation(dst, src, ACT.Copy).then_inc(ready, 1)

            def w_half(c):
                act.wait_ge(w_loaded[c], 16)
                round_hi(w_hi[:, c], ws[:, c], w_hi_ready)

            def x_half(t, c):
                if t == 0:
                    act.wait_ge(x0_loaded[c], 16)
                elif c == 0:
                    act.wait_ge(x_loaded[t], 16)
                    if t >= 2:
                        act.wait_ge(base_done, (t - 1) * K)
                round_hi(x_hi[:, t % 2, c], xs[:, t, c], x_hi_ready)

            def a1_half(g):
                act.wait_ge(rows_loaded[g], 16)
                if g >= SLOTS:
                    act.wait_ge(up_done, PARTS * (g // GPB - 1))
                s = g % SLOTS
                if packed(g):
                    if g >= GPB:
                        act.wait_ge(a1_lo_ready, g - GPB + 1)
                    round_hi(a1_hi[:, g % GPB], rows[:, s], a1_hi_ready)
                else:
                    round_hi(a1_ops[:, s, 0], rows[:, s], a1_hi_ready)

            def pack_a1(g):
                act.wait_ge(a1_lo_ready, g + 1)
                s = g % SLOTS
                for h, own in enumerate(halves):
                    nc.scalar.activation(a1_ops[own, s, h], a1_hi[own, g % GPB], ACT.Copy)
                    last = nc.scalar.activation(a1_ops[halves[1 - h], s, h], a1_rest[own, g % GPB], ACT.Copy)
                last.then_inc(a1_packed, 1)

            def exp_gap(u):
                act.wait_ge(gap_ready, u + 1)
                nc.scalar.activation(gap_exp[:], gap[:], ACT.Exp).then_inc(exp_ready, 1)

            def gt_half(u):
                act.wait_ge(gt_done, u + 1)
                if u >= 1:
                    act.wait_ge(lora_done, u * K)
                round_hi(gt_hi[:], side[1][:], gt_hi_ready)

            def down_half(g):
                act.wait_ge(down_ready, g + 1)
                if g >= SLOTS:
                    act.wait_ge(up_done, PARTS * (g // GPB - 1))
                s = g % SLOTS
                if packed(g):
                    for to in (0, 1):
                        for h, own in enumerate(halves):
                            last = nc.scalar.activation(down_ops[halves[h ^ to], s, h, 0:GT // 2],
                                                        down[own, g % GPB, 0:GT // 2], ACT.Copy)
                        last.then_inc(down_hi_ready, 1)
                else:
                    round_hi(down_ops[:, s, 0], down[:, g % GPB], down_hi_ready)

            for c in range(K):
                x_half(0, c)
            for c in range(1, K):
                w_half(c)
            act.wait_ge(b0_loaded, 16)
            round_hi(b0_hi[:], b0s[:], b0_hi_ready)
            exp_gap(0)
            for c in range(K):
                x_half(1, c)
            gt_half(0)
            for t in range(NB - 1):
                if t == 0:
                    for g in range(GPB):
                        a1_half(g)
                    for g in range(GPB):
                        pack_a1(g)
                exp_gap(t + 1)
                for g in range(t * GPB, (t + 1) * GPB):
                    down_half(g)
                gt_half(t + 1)
                for g in range((t + 1) * GPB, (t + 2) * GPB):
                    a1_half(g)
                if t + 2 < NB:
                    for c in range(K):
                        x_half(t + 2, c)
                    for g in range((t + 1) * GPB, (t + 2) * GPB):
                        pack_a1(g)
            for g in range((NB - 1) * GPB, NG):
                down_half(g)

        @block.vector
        def _(dve):
            steps = [0]

            def then_wait(instruction):
                steps[0] += 1
                instruction.then_inc(vector_step, 1)
                dve.wait_ge(vector_step, steps[0])

            def split_lo(dst, src, hi, ready):
                nc.vector.tensor_tensor(dst, src, hi.bitcast(F32), ALU.subtract).then_inc(ready, 1)

            def top_two(u):
                dve.wait_ge(aw_done, u + 1)
                for j, h in h_parts(u):
                    last = nc.vector.tensor_tensor(logits[:, j], h[:, :, H:AWN], bias[:, u, j], ALU.add)
                then_wait(last)
                for j in range(TILES):
                    last = nc.vector.max(top[:, j], logits[:, j])
                then_wait(last)
                nc.vector.tensor_tensor(gap[:], top[:, :, 1], top[:, :, 0], ALU.subtract).then_inc(gap_ready, 1)

            def pick():
                for j in range(TILES):
                    last = nc.vector.max_index(top_at[:, j], top[:, j], logits[:, j])
                then_wait(last)
                then_wait(nc.vector.tensor_tensor(
                    picked[:], top_at[:, :, 0:2].unsqueeze(3).broadcast_to([P, TILES, 2, experts]),
                    expert_no[:].unsqueeze(1).unsqueeze(1).broadcast_to([P, TILES, 2, experts]), ALU.is_equal))

            def gate_h(u):
                dve.wait_ge(exp_ready, u + 1)
                then_wait(nc.vector.tensor_scalar(denom[:], gap_exp[:], 1.0, None, ALU.add))
                then_wait(nc.vector.reciprocal(inv[:], denom[:]))
                nc.vector.tensor_scalar(weight[:, :, 0], inv[:], SCALING0, None, ALU.mult)
                then_wait(nc.vector.scalar_tensor_tensor(weight[:, :, 1], gap_exp[:], SCALING0, inv[:],
                                                         ALU.mult, ALU.mult))
                then_wait(nc.vector.tensor_tensor(
                    picked_w[:], picked[:], weight[:].unsqueeze(3).broadcast_to([P, TILES, 2, experts]), ALU.mult))
                then_wait(nc.vector.tensor_tensor(gate[:], picked_w[:, :, 0], picked_w[:, :, 1], ALU.add))
                if u >= 1:
                    dve.wait_ge(gt_done, u)
                for j, h in h_parts(u):
                    last = nc.vector.tensor_tensor(
                        gated[:, j].rearrange("p j (e r) -> p j e r", e=experts),
                        h[:, :, 0:H].rearrange("p j (e r) -> p j e r", e=experts),
                        gate[:, j].unsqueeze(3).broadcast_to([P, j.stop - j.start, experts, rank]), ALU.mult)
                    if j.stop in (TILES // 2, TILES):
                        last.then_inc(gated_ready, 1)

            def add_x1(t, c):
                dve.wait_ge(lora_done, t * K + c + 1)
                nc.vector.tensor_tensor(xs[:, t, c], main[c][:], xs[:, t, c], ALU.add).then_inc(x1_ready, 1)

            def add_x1_last(s):
                n = slice(s * GT, (s + 1) * GT)
                dve.wait_ge(lora_done, NB * K + s)
                nc.vector.tensor_tensor(xs[:, NB - 1, K - 1, n], last_x1_banks[s][:, 0:GT], xs[:, NB - 1, K - 1, n],
                                        ALU.add).then_inc(x1_ready, 1)

            def mask_down(g):
                dve.wait_ge(down_done, g + 1)
                tiles, own = (CT // 2, own_in_half) if packed(g) else (CT, own_batch)
                spread = [P, tiles, BPT, tokens_per_batch]
                nc.vector.tensor_tensor(
                    down[:, g % GPB, 0:tiles * NT].rearrange("p (j b n) -> p j b n", j=tiles, b=BPT),
                    side[g % 2][:, 0:NT].rearrange("p (b n) -> p b n", b=BPT).unsqueeze(1).broadcast_to(spread),
                    own[:].rearrange("p (j b) -> p j b", j=tiles).unsqueeze(3).broadcast_to(spread),
                    ALU.mult).then_inc(down_ready, 1)

            def down_rest(g):
                s = g % SLOTS
                if packed(g):
                    dve.wait_ge(down_hi_ready, 2 * g + 1)
                    for h, own in enumerate(halves):
                        last = nc.vector.tensor_tensor(
                            down_ops[own, s, h, GT // 2:], down[own, g % GPB, 0:GT // 2],
                            down_ops[own, s, h, 0:GT // 2].bitcast(F32), ALU.subtract)
                    last.then_inc(down_lo_ready, 1)
                else:
                    dve.wait_ge(down_hi_ready, NG - GPB + g + 1)
                    split_lo(down_ops[:, s, 1], down[:, g % GPB], down_ops[:, s, 0], down_lo_ready)

            def gt_rest(u):
                dve.wait_ge(gt_hi_ready, u + 1)
                split_lo(gt_lo[:], side[1][:], gt_hi[:], gt_lo_ready)

            def add_x2_last(s, c):
                n = slice(s * GT, (s + 1) * GT)
                dve.wait_ge(up_done, (NB - 1) * PARTS + s * K + c + 1)
                nc.vector.tensor_tensor(xs[:, NB - 1, c, n], last_banks[s * K + c][:, 0:GT], xs[:, NB - 1, c, n],
                                        ALU.add).then_inc(x2_ready, 1)

            def add_x2(t, parts):
                def one(i, part):
                    c, s = divmod(i, GPB)
                    to = xs[:, t, c, s * GT:(s + 1) * GT].rearrange("p (h n) -> p h n", h=2)
                    return nc.vector.tensor_tensor(
                        to, up_banks[i][:].rearrange("p (h q n) -> p h q n", h=2, q=2)[:, :, part], to, ALU.add)
                for i in parts:
                    dve.wait_ge(up_done, t * PARTS + i + 1)
                    last = one(i, 0)
                then_wait(last)
                for i in parts:
                    one(i, 1).then_inc(x2_ready, 1)

            nc.vector.memset(zeros[:], 0.0).then_inc(zeros_ready, 1)
            for c in range(K):
                dve.wait_ge(x_hi_ready, c + 1)
                split_lo(x_lo[:, 0, c], xs[:, 0, c], x_hi[:, 0, c], x0_lo_ready)
            dve.wait_ge(w_loaded[0], 16)
            nc.vector.tensor_copy(w_hi[:, 0], ws[:, 0]).then_inc(w0_hi_ready, 1)
            dve.wait_ge(w0_hi_ready, 1)
            split_lo(w_lo[:, 0], ws[:, 0], w_hi[:, 0], w0_lo_ready)
            dve.wait_ge(const_ready, 2)
            dve.wait_ge(adapter_loaded, 32)
            then_wait(nc.vector.tensor_scalar(rank_no[:], part_no[:], rank - 1, None, ALU.bitwise_and))
            then_wait(nc.vector.tensor_scalar(wrap[:], adapter_ids[:], 0.0, float(adapters), ALU.is_lt, ALU.mult))
            then_wait(nc.vector.tensor_tensor(wrapped[:], wrap[:], adapter_ids[:], ALU.add))
            then_wait(nc.vector.tensor_scalar(clamped[:], wrapped[:], 0.0, float(adapters - 1), ALU.max, ALU.min))
            nc.vector.scalar_tensor_tensor(row_at[:], clamped[:], float(rank), rank_no[:].broadcast_to([P, NG]),
                                           ALU.mult, ALU.add).then_inc(row_at_ready, 1)
            then_wait(nc.vector.tensor_scalar(row_wrap[:], adapter_row[:], 0.0, float(adapters), ALU.is_lt, ALU.mult))
            then_wait(nc.vector.tensor_tensor(row_wrapped[:], row_wrap[:], adapter_row[:], ALU.add))
            nc.vector.tensor_scalar(row_clamped[:], row_wrapped[:], 0.0, float(adapters - 1), ALU.max,
                                    ALU.min).then_inc(row_clamped_ready, 1)
            dve.wait_ge(language_loaded, 16)
            then_wait(nc.vector.tensor_tensor(
                is_language[:].rearrange("p t j e -> p (t j) e"),
                language_ids[:].rearrange("p t j -> p (t j)").unsqueeze(2).broadcast_to([P, NB * TILES, experts]),
                expert_no[:].unsqueeze(1).broadcast_to([P, NB * TILES, experts]), ALU.is_equal))
            then_wait(nc.vector.tensor_scalar(bias[:], is_language[:], LANG_BIAS, None, ALU.mult))
            for h in range(2):
                nc.vector.memset(down_ops[halves[1 - h], :, h, GT // 2:].bitcast(F32), 0.0).then_inc(pads_ready, 1)
            dve.wait_ge(b0_hi_ready, 1)
            split_lo(b0_lo[:], b0s[:], b0_hi[:], b0_lo_ready)
            top_two(0)
            pick()
            gate_h(0)
            gt_rest(0)
            dve.wait_ge(const_ready, 4)
            then_wait(nc.vector.tensor_tensor(own_in_half[:], own_batch[:, 0:BPG // 2], own_batch[:, BPG // 2:],
                                              ALU.add))
            for t in range(NB):
                more = t + 1 < NB
                for c in range(K):
                    if c == 2 and t >= 1:
                        add_x2(t - 1, range(EARLY, PARTS))
                    if c == (K - 1 if t else 1) and more:
                        top_two(t + 1)
                    if more or c < K - 1:
                        add_x1(t, c)
                if more:
                    pick()
                    for g in range(t * GPB, (t + 1) * GPB):
                        mask_down(g)
                    gate_h(t + 1)
                    for g in range(t * GPB, (t + 1) * GPB):
                        down_rest(g)
                    gt_rest(t + 1)
                    for i in range(0, EARLY, 2):
                        add_x2(t, range(i, min(i + 2, EARLY)))
            add_x1_last(0)
            mask_down(NG - 2)
            add_x1_last(1)
            down_rest(NG - 2)
            mask_down(NG - 1)
            for i in range(GPB * K):
                if i == 2:
                    down_rest(NG - 1)
                add_x2_last(*divmod(i, K))

        @block.tensor
        def _(pe):
            def base(t, c):
                if c == 0:
                    pe.wait_ge(w0_hi_ready, 1)
                else:
                    pe.wait_ge(w_hi_ready, c)
                if t >= 1:
                    if c < 2:
                        pe.wait_ge(x1_ready, (t - 1) * K + c + 1)
                    else:
                        pe.wait_ge(x2_ready, (t - 1) * PARTS + c - 1)
                base_products(t, c, main[c][:], slice(0, TB))

            def base_products(t, c, out_ap, n):
                s = t % 2
                for k in range(K):
                    if c == 0:
                        pe.wait_ge(x_hi_ready, t * K + k + 1)
                    nc.tensor.matmul(out_ap, w_hi[:, c, k], x_hi[:, s, k, n], start=(k == 0), stop=False)
                if c == 0:
                    pe.wait_ge(w0_lo_ready, 1)
                else:
                    pe.wait_ge(w_lo_ready, c)
                for k in range(K):
                    nc.tensor.matmul(out_ap, w_lo[:, c, k], x_hi[:, s, k, n], start=False, stop=False)
                for k in range(K):
                    if t == 0 and c == 0:
                        pe.wait_ge(x0_lo_ready, k + 1)
                    elif c == 0:
                        pe.wait_ge(x_lo_ready, (t - 1) * K + k + 1)
                    last = nc.tensor.matmul(out_ap, w_hi[:, c, k], x_lo[:, s, k, n], start=False, stop=False)
                last.then_inc(base_done, 1)

            def lora(t, c):
                if c == 0:
                    pe.wait_ge(gt_hi_ready, t + 1)
                    pe.wait_ge(b0_hi_ready, 1)
                    pe.wait_ge(b0_lo_ready, 1)
                    pe.wait_ge(gt_lo_ready, t + 1)
                lora_products(c, main[c][:], slice(0, TB))

            def lora_products(c, out_ap, n):
                m = slice(c * P, (c + 1) * P)
                nc.tensor.matmul(out_ap, b0_hi[:, m], gt_hi[:, n], start=False, stop=False)
                nc.tensor.matmul(out_ap, b0_lo[:, m], gt_hi[:, n], start=False, stop=False)
                nc.tensor.matmul(out_ap, b0_hi[:, m], gt_lo[:, n], start=False, stop=True).then_inc(lora_done, 1)

            def base_last(s):
                pe.wait_ge(x2_ready, (NB - 2) * PARTS + (K - 2 if s == 0 else PARTS - 1))
                base_products(NB - 1, K - 1, last_x1_banks[s][:, 0:GT], slice(s * GT, (s + 1) * GT))

            def lora_last(s):
                lora_products(K - 1, last_x1_banks[s][:, 0:GT], slice(s * GT, (s + 1) * GT))

            def aw_product(u, j, k):
                h = [h[:, j - js.start] for js, h in h_parts(u) if js.start <= j < js.stop][0]
                return nc.tensor.matmul(h, xs[:, u, k, j * P:(j + 1) * P], aws[:, k], start=(k == 0), stop=(k == K - 1))

            def aw_first():
                for k in range(K):
                    if k <= 1:
                        pe.wait_ge(aw_loaded[k], 16)
                    pe.wait_ge(x0_loaded[k], 16)
                    for j in range(TILES):
                        last = aw_product(0, j, k)
                last.then_inc(aw_done, 1)

            def aw_tiles(u):
                pe.wait_ge(x_loaded[u], 16)
                pe.wait_ge(gated_ready, u * 2)
                if u >= 2:
                    pe.wait_ge(x2_ready, (u - 1) * PARTS)
                for j in range(TILES):
                    for k in range(K):
                        last = aw_product(u, j, k)
                last.then_inc(aw_done, 1)

            def gt_transposes(u):
                pe.wait_ge(gated_ready, u * 2 + 1)
                if u == 0:
                    pe.wait_ge(const_ready, 3)
                else:
                    pe.wait_ge(down_ready, u * GPB)
                for j in range(TILES):
                    if j == TILES // 2:
                        pe.wait_ge(gated_ready, u * 2 + 2)
                    last = nc.tensor.transpose(side[1][:, j * P:(j + 1) * P], gated[:, j], ident[:])
                last.then_inc(gt_done, 1)

            def down_part(g, k):
                t, s = g // GPB, g % GPB
                if t == NB - 1 and k == K - 1:
                    pe.wait_ge(x1_ready, NB * K + s)
                else:
                    pe.wait_ge(x1_ready, t * K + k + 1)
                if k == 0:
                    pe.wait_ge(b1_loaded[g], 16 * BPG)
                    if s == 1:
                        pe.wait_ge(gt_lo_ready, t + 1)
                    elif t >= 1:
                        pe.wait_ge(x2_ready, t * PARTS)
                for j in range(CT):
                    n = s * GT + j * NT
                    last = nc.tensor.matmul(side[s][j * CW:(j + 1) * CW, 0:NT], b1s[:, g, j * CW:(j + 1) * CW, k],
                                            xs[:, t, k, n:n + NT], start=(k == 0), stop=(k == K - 1),
                                            tile_position=(0, j * CW))
                if k == K - 1:
                    last.then_inc(down_done, 1)

            def up(t, i):
                bank = up_banks[i]
                c, s = divmod(i, GPB)
                g, a = t * GPB + s, (t * GPB + s) % SLOTS
                if i < GPB:
                    pe.wait_ge(a1_packed, g + 1)
                    pe.wait_ge(down_hi_ready, 2 * g + 2)
                    pe.wait_ge(down_lo_ready, g + 1)
                    pe.wait_ge(pads_ready, 2)
                if bank in main:
                    pe.wait_ge(x1_ready, t * K + main.index(bank) + 1)
                if i >= EARLY:
                    pe.wait_ge(x2_ready, t * PARTS + up_banks.index(bank) + 1)
                for h in range(2):
                    last = nc.tensor.matmul(bank[:, h * GT:(h + 1) * GT], a1_ops[:, a, h, c * P:(c + 1) * P],
                                            down_ops[:, a, h], start=True, stop=True)
                last.then_inc(up_done, 1)

            def up_last(s, c):
                g, a, m = NG - GPB + s, (NG - GPB + s) % SLOTS, slice(c * P, (c + 1) * P)
                bank = last_banks[s * K + c]
                if c == 0:
                    pe.wait_ge(a1_lo_ready, g + 1)
                    pe.wait_ge(down_hi_ready, NG - GPB + g + 1)
                nc.tensor.matmul(bank[:, 0:GT], a1_ops[:, a, 0, m], down_ops[:, a, 0], start=True, stop=False)
                nc.tensor.matmul(bank[:, 0:GT], a1_ops[:, a, 1, m], down_ops[:, a, 0], start=False, stop=False)
                if c == 0:
                    pe.wait_ge(down_lo_ready, g + 1)
                nc.tensor.matmul(bank[:, 0:GT], a1_ops[:, a, 0, m], down_ops[:, a, 1], start=False, stop=True)\
                  .then_inc(up_done, 1)

            pe.wait_ge(zeros_ready, 1)
            for _ in range(WARM):
                nc.tensor.matmul(main[0][:], zeros[:, 0:P], zeros[:], start=True, stop=True)
            aw_first()
            base(0, 0)
            base(0, 1)
            base(0, 2)
            gt_transposes(0)
            base(0, 3)
            for c in range(K):
                if c == 1:
                    aw_tiles(1)
                lora(0, c)
            for t in range(NB - 1):
                for k in range(K - 1):
                    down_part(t * GPB, k)
                    down_part(t * GPB + 1, k)
                down_part(t * GPB, K - 1)
                down_part(t * GPB + 1, K - 1)
                base(t + 1, 0)
                gt_transposes(t + 1)
                base(t + 1, 1)
                for i in range(EARLY):
                    up(t, i)
                lora(t + 1, 0)
                lora(t + 1, 1)
                base(t + 1, 2)
                for i in range(EARLY, PARTS):
                    up(t, i)
                lora(t + 1, 2)
                if t + 2 < NB:
                    base(t + 1, 3)
                    aw_tiles(t + 2)
                    lora(t + 1, 3)
            base_last(0)
            lora_last(0)
            for k in range(K - 1):
                down_part(NG - 2, k)
            base_last(1)
            down_part(NG - 2, K - 1)
            lora_last(1)
            for k in range(K):
                down_part(NG - 1, k)
            for i in range(GPB * K):
                up_last(*divmod(i, K))


def kernel(x, itok_B_0_7, itok_B_4_50, L0_cond_W, L0_cond_Wr, L0_cond_A, L0_cond_B, L1_cond_A, L1_cond_B):
    import numpy as np
    import concourse.bacc as bacc
    from concourse.bass_utils import run_bass_kernel_spmd

    x, w, wr, a0, b0, a1, b1 = (np.asarray(v) for v in (
        x, L0_cond_W, L0_cond_Wr, L0_cond_A, L0_cond_B, L1_cond_A, L1_cond_B))
    adapter, language = np.asarray(itok_B_4_50), np.asarray(itok_B_0_7)
    B, T, D = x.shape
    E, R, _ = a0.shape
    NA = a1.shape[0]
    K, TB = D // P, 512
    NB = B * T // TB
    arrays = {
        "x_t": x.reshape(NB, TB, K, P).transpose(3, 0, 2, 1),
        "adapter_id": np.repeat(adapter.reshape(-1, P // R).T, R, axis=0),
        "adapter_list": adapter.reshape(1, B),
        "language_id": np.repeat(language.reshape(-1, P // T).T, T, axis=0),
        "w_t": w.reshape(K, P, K, P).transpose(3, 0, 2, 1),
        "aw_t": np.concatenate([a0.reshape(E * R, D), wr]).T.reshape(K, P, -1).transpose(1, 0, 2),
        "b0_t": b0.transpose(0, 2, 1).reshape(E * R, D),
        "a1_t": a1.transpose(0, 2, 1).reshape(NA * R, D),
        "b1_t": b1.reshape(NA, R, K, P).transpose(0, 3, 1, 2).reshape(NA, P, R * K),
    }
    arrays = {k: np.ascontiguousarray(v) for k, v in arrays.items()}

    nc = bacc.Bacc("TRN2", target_bir_lowering=False, num_devices=1)
    aps = [nc.dram_tensor(k, v.shape, mybir.dt.from_np(v.dtype), kind="ExternalInput").ap() for k, v in arrays.items()]
    out = nc.dram_tensor("out_t", arrays["x_t"].shape, F32, kind="ExternalOutput").ap()
    two_block_kernel(nc, *aps, out, tokens_per_batch=T, experts=E, rank=R, adapters=NA)
    r = run_bass_kernel_spmd(nc, [arrays], core_ids=[0])
    return r.results[0]["out_t"].transpose(1, 3, 2, 0).reshape(B, T, D)
```
